# Optimizing a Trainium2 kernel written in Bass

```python
import numpy as np
import jax
import jax.numpy as jnp

def _softmax(x, axis=-1):
    return jax.nn.softmax(x, axis=axis)

def _gelu(x):
    return jax.nn.gelu(x, approximate=True)

def _silu(x):
    return jax.nn.silu(x)

def _sigmoid(x):
    return jax.nn.sigmoid(x)

def _layernorm(x, axis=-1, eps=1e-05):
    m = jnp.mean(x, axis=axis, keepdims=True)
    v = jnp.var(x, axis=axis, keepdims=True)
    return (x - m) / jnp.sqrt(v + eps)

def _scatter_add(tgt, idx, src, axis=0):
    return tgt.at[idx].add(src)

def _segment_sum(src, seg, n):
    return jax.ops.segment_sum(src, seg, n)
kernel_name = 'mk_seq_preln_d1_jaxref_r8_62a4be'

def setup_inputs(seed: int=0):
    np.random.seed(seed)
    _w = jnp.asarray

    def _L0_attn_setup():
        import jax, jax.numpy as jnp
        import numpy as np
        import math
        NUM_BUCKETS = 32
        MAX_DISTANCE = 128
        N_HEADS = 16
        D_KV = 64

        def _relative_position_bucket(relative_position, num_buckets=NUM_BUCKETS, max_distance=MAX_DISTANCE):
            num_buckets //= 2
            relative_buckets = (relative_position > 0).astype(jnp.int32) * num_buckets
            rp = jnp.abs(relative_position)
            max_exact = num_buckets // 2
            is_small = rp < max_exact
            rp_large = max_exact + (jnp.log(jnp.maximum(rp, 1).astype(jnp.float32) / max_exact) / math.log(max_distance / max_exact) * (num_buckets - max_exact)).astype(jnp.int32)
            rp_large = jnp.minimum(rp_large, num_buckets - 1)
            return relative_buckets + jnp.where(is_small, rp, rp_large)

        def compute_bias(rel_bias, q_len, k_len):
            ctx = jnp.arange(q_len)[:, None]
            mem = jnp.arange(k_len)[None, :]
            buckets = _relative_position_bucket(mem - ctx)
            values = rel_bias[buckets]
            return jnp.transpose(values, (2, 0, 1))[None]
        key = jax.random.key(seed)
        ks = jax.random.split(key, 6)
        d_model, inner = (128, N_HEADS * D_KV)
        s = 0.02
        return {'hidden_states': jax.random.normal(ks[0], (2, 256, d_model), jnp.float32), 'Wq': jax.random.normal(ks[1], (d_model, inner), jnp.float32) * s, 'Wk': jax.random.normal(ks[2], (d_model, inner), jnp.float32) * s, 'Wv': jax.random.normal(ks[3], (d_model, inner), jnp.float32) * s, 'Wo': jax.random.normal(ks[4], (inner, d_model), jnp.float32) * s, 'rel_bias': jax.random.normal(ks[5], (NUM_BUCKETS, N_HEADS), jnp.float32) * s}
    _L0_attn_in = _L0_attn_setup()

    def _L0_ffn_setup():
        import jax, jax.numpy as jnp
        import numpy as np
        B, L, D = (4, 64, 128)
        E, TOP_K = (16, 4)
        F = 4 * D
        key = jax.random.key(seed)
        ks = jax.random.split(key, 6)
        scale = 0.02
        return {'x': jax.random.normal(ks[0], (B, L, D), jnp.float32), 'keys': jax.random.normal(ks[1], (E, D), jnp.float32), 'w1': jax.random.normal(ks[2], (E, F, D), jnp.float32) * scale, 'b1': jnp.zeros((E, F), jnp.float32), 'w2': jax.random.normal(ks[3], (E, D, F), jnp.float32) * scale, 'b2': jnp.zeros((E, D), jnp.float32), 'rw': jax.random.normal(ks[4], (E, D), jnp.float32) * scale, 'rb': jnp.zeros((E,), jnp.float32)}
    _L0_ffn_in = _L0_ffn_setup()
    _d = {'L0_attn_hidden_states': _L0_attn_in['hidden_states'], 'L0_attn_Wq': _L0_attn_in['Wq'], 'L0_attn_Wk': _L0_attn_in['Wk'], 'L0_attn_Wv': _L0_attn_in['Wv'], 'L0_attn_Wo': _L0_attn_in['Wo'], 'L0_attn_rel_bias': _L0_attn_in['rel_bias'], 'L0_ffn_keys': _L0_ffn_in['keys'], 'L0_ffn_w1': _L0_ffn_in['w1'], 'L0_ffn_b1': _L0_ffn_in['b1'], 'L0_ffn_w2': _L0_ffn_in['w2'], 'L0_ffn_b2': _L0_ffn_in['b2'], 'L0_ffn_rw': _L0_ffn_in['rw'], 'L0_ffn_rb': _L0_ffn_in['rb']}
    _x0 = _d['L0_attn_hidden_states']
    _d['L0_attn_hidden_states'] = jax.random.normal(jax.random.fold_in(jax.random.key(seed), 1), (8, 512, 128), dtype=_x0.dtype)
    del _x0
    return _d

def reference(L0_attn_hidden_states, L0_attn_Wq, L0_attn_Wk, L0_attn_Wv, L0_attn_Wo, L0_attn_rel_bias, L0_ffn_keys, L0_ffn_w1, L0_ffn_b1, L0_ffn_w2, L0_ffn_b2, L0_ffn_rw, L0_ffn_rb):

    def _L0_attn_ref(hidden_states, Wq, Wk, Wv, Wo, rel_bias):
        import jax, jax.numpy as jnp
        import numpy as np
        import math
        NUM_BUCKETS = 32
        MAX_DISTANCE = 128
        N_HEADS = 16
        D_KV = 64

        def _relative_position_bucket(relative_position, num_buckets=NUM_BUCKETS, max_distance=MAX_DISTANCE):
            num_buckets //= 2
            relative_buckets = (relative_position > 0).astype(jnp.int32) * num_buckets
            rp = jnp.abs(relative_position)
            max_exact = num_buckets // 2
            is_small = rp < max_exact
            rp_large = max_exact + (jnp.log(jnp.maximum(rp, 1).astype(jnp.float32) / max_exact) / math.log(max_distance / max_exact) * (num_buckets - max_exact)).astype(jnp.int32)
            rp_large = jnp.minimum(rp_large, num_buckets - 1)
            return relative_buckets + jnp.where(is_small, rp, rp_large)

        def compute_bias(rel_bias, q_len, k_len):
            ctx = jnp.arange(q_len)[:, None]
            mem = jnp.arange(k_len)[None, :]
            buckets = _relative_position_bucket(mem - ctx)
            values = rel_bias[buckets]
            return jnp.transpose(values, (2, 0, 1))[None]
        B, S, D = hidden_states.shape

        def split_heads(x):
            return x.reshape(B, S, N_HEADS, D_KV).transpose(0, 2, 1, 3)
        q = split_heads(hidden_states @ Wq)
        k = split_heads(hidden_states @ Wk)
        v = split_heads(hidden_states @ Wv)
        scores = jnp.einsum('bhqd,bhkd->bhqk', q, k)
        scores = scores + compute_bias(rel_bias, S, S)
        attn = jax.nn.softmax(scores, axis=-1)
        ctx = jnp.einsum('bhqk,bhkd->bhqd', attn, v)
        ctx = ctx.transpose(0, 2, 1, 3).reshape(B, S, N_HEADS * D_KV)
        return ctx @ Wo

    def _L0_ffn_ref(x, keys, w1, b1, w2, b2, rw, rb):
        import jax, jax.numpy as jnp
        import numpy as np
        B, L, D = (4, 64, 128)
        E, TOP_K = (16, 4)
        F = 4 * D
        diff = x[:, :, None, :] - keys
        dist2 = jnp.sum(diff * diff, axis=-1)
        logits = -dist2 + jnp.einsum('bld,ed->ble', x, rw) + rb
        topv, topi = jax.lax.top_k(logits, TOP_K)
        w = jax.nn.softmax(topv, axis=-1)
        hidden = jax.nn.gelu(jnp.einsum('bld,efd->blef', x, w1) + b1, approximate=False)
        exp_out = jnp.einsum('blef,edf->bled', hidden, w2) + b2
        sel = jnp.take_along_axis(exp_out, topi[..., None], axis=2)
        fused = jnp.sum(w[..., None] * sel, axis=2)
        return fused
    x = L0_attn_hidden_states
    x = x + _L0_attn_ref(_layernorm(x, axis=-1), L0_attn_Wq, L0_attn_Wk, L0_attn_Wv, L0_attn_Wo, L0_attn_rel_bias)
    x = x + _L0_ffn_ref(_layernorm(x, axis=-1), L0_ffn_keys, L0_ffn_w1, L0_ffn_b1, L0_ffn_w2, L0_ffn_b2, L0_ffn_rw, L0_ffn_rb)
    return x

_drawn_inputs = setup_inputs


def setup_inputs(seed=0):
    import zlib

    import numpy as np

    out = dict(_drawn_inputs(seed))
    spreads = {'L0_ffn_b1': (0.0, 1.648), 'L0_ffn_b2': (0.0, 0.433), 'L0_ffn_rb': (0.0, 2.0)}
    factors = {'L0_attn_Wq': 8.0,
     'L0_attn_Wk': 8.0,
     'L0_attn_Wv': 6.119,
     'L0_attn_Wo': 6.143,
     'L0_attn_rel_bias': 8.0,
     'L0_ffn_rw': 64.0,
     'L0_ffn_w1': 5.314,
     'L0_ffn_w2': 2.98}
    for name, (base, spread) in spreads.items():
        noise = np.random.default_rng([zlib.crc32(name.encode()), seed]).standard_normal(out[name].shape)
        drawn = base * np.exp(spread * noise) if base else spread * noise
        out[name] = jnp.asarray(drawn.astype(out[name].dtype))
    for name, factor in factors.items():
        out[name] = (out[name] * factor).astype(out[name].dtype)
    return out
```

```python
from contextlib import ExitStack

import concourse.bass as bass
from concourse import mybir

F32 = mybir.dt.float32
F32R = mybir.dt.float32r
U32 = mybir.dt.uint32
ALU = mybir.AluOpType
ACT = mybir.ActivationFunctionType

P = 128
DH = 64
TC = 4
EPS = 1e-5
BIG = 3.0e38


def layer_kernel(nc, x, wq, wk, wv, wo, rel_bias, onehot, ident, flip, expert_no, w1t, b1t, w2t, b2, keys_t, rw_t, rb, out):
    T, D = x.shape
    S = TC * P
    NB = T // S
    NCH = T // P
    H = wq.shape[1] // DH
    NPR = H // 2
    NE = rb.shape[1]
    FC = b1t.shape[1] // NE
    NBUCKET = rel_bias.shape[0]
    ROLL = 2 * S
    STRIP = S + (TC - 1) * P

    with ExitStack() as ctx:
        def sb(name, shape, dt=F32, stack=ctx):
            return stack.enter_context(nc.sbuf_tensor(name, shape, dt))

        def sem(name):
            return ctx.enter_context(nc.semaphore(name))

        def bank(name):
            return ctx.enter_context(nc.psum_tensor(name, [P, 512], F32))

        x_all = sb("x_all", [P, NCH + TC, D])
        idn = sb("idn", [P, P])
        minus_half = sb("minus_half", [P, TC])
        stats = sb("stats", [P, TC, 6])
        moments = sb("moments", [P, TC, 2])
        var_eps = sb("var_eps", [P, TC])
        rstd = sb("rstd", [P, TC])
        xn = sb("xn", [P, TC, D])
        xnt_hi = sb("xnt_hi", [P, S], F32R)
        xnt_lo = sb("xnt_lo", [P, S], F32R)

        attn = ctx.enter_context(ExitStack())
        stage = sb("stage", [P, H * DH], stack=attn)
        w_hi = [sb(f"w{n}_hi", [P, H * DH], F32R, attn) for n in "kqv"]
        w_lo = [sb(f"w{n}_lo", [P, H * DH], F32R, attn) for n in "kqv"]
        wo_sb = sb("wo_sb", [P, NPR, D], stack=attn)
        rb_sb = sb("rb_sb", [NBUCKET, H], stack=attn)
        strips = sb("strips", [P, H, STRIP], stack=attn)
        q_st = sb("q_st", [P, 2, 2, S], F32R, attn)
        k_st = sb("k_st", [P, 2, 2, S], F32R, attn)
        k_sw = sb("k_sw", [P, 2, 2, S], F32R, attn)
        v_sb = sb("v_sb", [P, 2, TC, P], stack=attn)
        neg = sb("neg", [P, TC, S], stack=attn)
        nmax = sb("nmax", [P, 2 * TC], stack=attn)
        prob = sb("prob", [P, 2, 2, TC, S], stack=attn)
        rsum = sb("rsum", [P, 2 * TC], stack=attn)
        rinv = sb("rinv", [P, 2 * TC], stack=attn)
        probt = sb("probt", [P, 2, TC, S], stack=attn)
        ctxt = sb("ctxt", [P, 2, S], stack=attn)
        flip_sb = neg[:, 0, 0:P]
        raw_strips = prob[:].rearrange("p g h c s -> p g (h c s)")
        onehot_sb = prob[0:NBUCKET, 0, 0, 0:2, :]
        roll_sb = prob[0:H, 0, 1, 0:2, :]

        roll_dram = nc.dram_tensor("roll_dram", [H, ROLL], F32, kind="Internal").ap()

        ps_prj = [bank("ps_prj0"), bank("ps_prj1")]
        ps_s = [bank("ps_s0"), bank("ps_s1")]
        ps_t = [bank("ps_t0"), bank("ps_t1")]
        ps_c = bank("ps_c")
        ps_o = bank("ps_o")

        ld_x0, ld_x, ld_c, ld_w = sem("ld_x0"), sem("ld_x"), sem("ld_c"), [sem(f"ld_w{n}") for n in "kqv"]
        ld_wo, ld_strip, roll_st = sem("ld_wo"), [sem(f"ld_strip{g}") for g in range(H // TC)], sem("roll_st")
        w_hi_rdy, w_lo_rdy = sem("w_hi_rdy"), sem("w_lo_rdy")
        roll_mm, roll_cp = sem("roll_mm"), sem("roll_cp")
        flip_rdy, strip_act, strip_dve = sem("flip_rdy"), sem("strip_act"), sem("strip_dve")
        half_rdy = sem("half_rdy")
        st_rdy, ve_rdy, rstd_rdy, xn_rdy = sem("st_rdy"), sem("ve_rdy"), sem("rstd_rdy"), sem("xn_rdy")
        mv_rdy = sem("mv_rdy")
        xt_rdy, xhi_rdy, xlo_rdy = sem("xt_rdy"), sem("xhi_rdy"), sem("xlo_rdy")
        k_rdy, q_rdy, v_rdy = sem("k_rdy"), sem("q_rdy"), sem("v_rdy")
        hi_rdy, lo_rdy, ksw_rdy, v_cp = sem("hi_rdy"), sem("lo_rdy"), sem("ksw_rdy"), sem("v_cp")
        s_rdy, neg_rdy, exp_rdy, rinv_rdy, norm_rdy = (sem(n) for n in
                                                       ("s_rdy", "neg_rdy", "exp_rdy", "rinv_rdy", "norm_rdy"))
        t_rdy, pt_act, pt_dve = sem("t_rdy"), sem("pt_act"), sem("pt_dve")
        c_rdy, c_cp, o_rdy, res_rdy = sem("c_rdy"), sem("c_cp"), sem("o_rdy"), sem("res_rdy")
        st_out = sem("st_out")

        strip_bank = [ps_s, ps_t]

        CHUNKS = H * TC
        HALVES = 4 * NPR

        def pair_halves(i):
            return [(ps_prj[(3 * i) % 2], k_st, 0), (ps_prj[(3 * i) % 2], k_st, 1),
                    (ps_prj[(3 * i + 1) % 2], q_st, 0), (ps_prj[(3 * i + 1) % 2], q_st, 1)]

        phase = ctx.enter_context(ExitStack())
        block = phase.enter_context(nc.Block())

        @block.sync
        def _(sp):
            sp.dma_start(x_all[:, 0:TC, :], x[0:S].rearrange("(n p) d -> p n d", p=P)).then_inc(ld_x0, 16)
            sp.dma_start(idn[:], ident).then_inc(ld_c, 16)
            sp.dma_start(stage[:], wk).then_inc(ld_w[0], 16)
            sp.dma_start(flip_sb, flip).then_inc(ld_c, 16)
            sp.dma_start(rb_sb[:], rel_bias).then_inc(ld_c, 16)
            sp.dma_start(onehot_sb, onehot.rearrange("n (a m) -> n a m", a=2)).then_inc(ld_c, 16)
            for n, w in ((1, wq), (2, wv)):
                sp.wait_ge(w_lo_rdy, n)
                sp.dma_start(stage[:], w).then_inc(ld_w[n], 16)
            sp.dma_start(wo_sb[:], wo.rearrange("(n p) d -> p n d", p=P)).then_inc(ld_wo, 16)
            sp.wait_ge(roll_cp, 2)
            sp.dma_start(roll_dram.rearrange("h (a m) -> h a m", a=2), roll_sb).then_inc(roll_st, 16)
            sp.wait_ge(roll_st, 16)
            for h in range(H):
                g, a = h // TC, h % TC
                if g >= 2 and a == 0:
                    sp.wait_ge(flip_rdy, 2 * TC * (g - 1))
                sp.dma_start(raw_strips[:, g % 2, a * STRIP:(a + 1) * STRIP],
                             bass.AP(roll_dram.tensor, h * ROLL, [[1, P], [1, STRIP]])).then_inc(ld_strip[g], 16)
            for n in range(1, NB):
                sp.dma_start(x_all[:, n * TC:(n + 1) * TC, :],
                             x[n * S:(n + 1) * S].rearrange("(n p) d -> p n d", p=P)).then_inc(ld_x, 16)
            sp.dma_start(x_all[:, NCH:NCH + TC, :], x[0:S].rearrange("(n p) d -> p n d", p=P)).then_inc(ld_x, 16)

            def swap_keys(b, i):
                g = i % 2
                sp.wait_ge(lo_rdy, b * HALVES + 4 * i + 2)
                sp.dma_start(k_sw[0:DH, g].bitcast(F32), k_st[DH:P, g].bitcast(F32)).then_inc(ksw_rdy, 16)
                sp.dma_start(k_sw[DH:P, g].bitcast(F32), k_st[0:DH, g].bitcast(F32)).then_inc(ksw_rdy, 16)

            swap_keys(0, 0)
            with sp.Fori(0, NB) as b:
                for i in range(1, NPR):
                    swap_keys(b, i)
                swap_keys(b + 1, 0)
            sp.wait_ge(ksw_rdy, 32 * (NB * NPR + 1))

        @block.gpsimd
        def _(pool):
            pool.memset(minus_half[:], -0.5).then_inc(half_rdy, 1)
            pool.wait_ge(half_rdy, 1)

            def rsqrt(n):
                pool.wait_ge(ve_rdy, n + 1)
                pool.tensor_tensor(rstd[:], var_eps[:], minus_half[:], ALU.pow).then_inc(rstd_rdy, 1)

            rsqrt(0)
            with pool.Fori(0, NB) as b:
                for i in range(NPR):
                    if i == 4:
                        rsqrt(b + 1)
                    for n in range(2 * TC):
                        pool.wait_ge(rinv_rdy, b * CHUNKS + 2 * TC * i + n + 1)
                        pool.nop(nofuse=True)
                        tile = prob[:, i % 2, n // TC, n % TC, :]
                        pool.tensor_scalar(tile, tile, rinv[:, n:n + 1], 1.0, ALU.mult, ALU.mult).then_inc(norm_rdy, 1)

        @block.scalar
        def _(act):
            for n in range(3):
                act.wait_ge(ld_w[n], 16)
                act.activation(w_hi[n][:], stage[:], ACT.Copy).then_inc(w_hi_rdy, 1)
                if n == 0:
                    for a in range(2):
                        act.wait_ge(roll_mm, a + 1)
                        act.activation(roll_sb[:, a, :], ps_s[a][0:H, :], ACT.Copy).then_inc(roll_cp, 1)

            def tokens_hi(n):
                act.wait_ge(xt_rdy, n + 1)
                act.activation(xnt_hi[:], ps_c[:], ACT.Copy).then_inc(xhi_rdy, 1)

            def split_hi(b, i, m):
                src, dst, hh = pair_halves(i)[m]
                act.wait_ge(k_rdy if m < 2 else q_rdy, b * NPR + i + 1)
                act.activation(dst[0:DH, i % 2, hh, :], src[DH * hh:DH * hh + DH, :], ACT.Copy).then_inc(hi_rdy, 1)

            def values(b, i):
                act.wait_ge(v_rdy, b * NPR + i + 1)
                act.activation(v_sb[:, i % 2].rearrange("p c d -> p (c d)"), ps_prj[(3 * i + 2) % 2][:],
                               ACT.Copy).then_inc(v_cp, 1)

            def exps(b, i, n):
                act.wait_ge(neg_rdy, b * CHUNKS + 2 * TC * i + n + 1)
                act.activation(prob[:, i % 2, n // TC, n % TC, :], neg[:, n % TC, :], ACT.Exp,
                               bias=nmax[:, n:n + 1], scale=-1.0, accum_out=rsum[:, n:n + 1]).then_inc(exp_rdy, 1)

            def weights_t(b, i, hh, j):
                act.wait_ge(t_rdy, b * CHUNKS + 2 * TC * i + TC * hh + j + 1)
                act.activation(probt[:, hh, j, :], ps_t[j % 2][:], ACT.Copy).then_inc(pt_act, 1)

            def context(b, i):
                act.wait_ge(c_rdy, b * NPR + i + 1)
                act.activation(ctxt[:, i % 2, :], ps_c[:], ACT.Copy).then_inc(c_cp, 1)

            tokens_hi(0)
            for m in range(4):
                split_hi(0, 0, m)
            values(0, 0)
            for h in range(H):
                act.wait_ge(flip_rdy, 2 * h + 1)
                act.activation(strips[:, h, 0:STRIP // 2], strip_bank[h % 2][0][:, 0:STRIP // 2], ACT.Copy)\
                    .then_inc(strip_act, 1)
            with act.Fori(0, NB) as b:
                for i in range(NPR):
                    for c in range(TC):
                        exps(b, i, c)
                        if i:
                            weights_t(b, i - 1, c // 2, 2 * (c % 2) + 1)
                    for c in range(TC):
                        if i + 1 < NPR:
                            split_hi(b, i + 1, c)
                        exps(b, i, TC + c)
                    if i:
                        context(b, i - 1)
                    if i + 1 < NPR:
                        values(b, i + 1)
                tokens_hi(b + 1)
                weights_t(b, NPR - 1, 0, 1)
                weights_t(b, NPR - 1, 0, 3)
                for m in range(4):
                    split_hi(b + 1, 0, m)
                weights_t(b, NPR - 1, 1, 1)
                weights_t(b, NPR - 1, 1, 3)
                values(b + 1, 0)
                context(b, NPR - 1)

        @block.vector
        def _(dve):
            def moments_of(n, first):
                for c in range(TC):
                    dve.bn_stats(stats[:, c, :], x_all[:, bass.ds(first + c, 1), :]).then_inc(st_rdy, 1)
                dve.wait_ge(st_rdy, (n + 1) * TC)
                dve.nop(nofuse=True)
                for c in range(TC):
                    dve.bn_aggr(moments[:, c, :], stats[:, c, :]).then_inc(mv_rdy, 1)
                dve.wait_ge(mv_rdy, (n + 1) * TC)
                dve.tensor_scalar(var_eps[:], moments[:, :, 1], EPS, None, ALU.add).then_inc(ve_rdy, 1)

            def normalise(n, first):
                dve.wait_ge(rstd_rdy, n + 1)
                for c in range(TC):
                    dve.tensor_scalar(xn[:, c, :], x_all[:, bass.ds(first + c, 1), :], moments[:, c, 0:1],
                                      rstd[:, c:c + 1], ALU.subtract, ALU.mult).then_inc(xn_rdy, 1)

            def tokens_lo(n):
                dve.wait_ge(xhi_rdy, n + 1)
                dve.tensor_tensor(xnt_lo[:], ps_c[:], xnt_hi[:].bitcast(F32), ALU.subtract).then_inc(xlo_rdy, 1)

            def split_lo(b, i, m):
                src, dst, hh = pair_halves(i)[m]
                dve.wait_ge(hi_rdy, b * HALVES + 4 * i + m + 1)
                dve.tensor_tensor(dst[DH:P, i % 2, hh, :], src[DH * hh:DH * hh + DH, :],
                                  dst[0:DH, i % 2, hh, :].bitcast(F32), ALU.subtract).then_inc(lo_rdy, 1)

            def scores(b, i, n):
                c = n % TC
                dve.wait_ge(s_rdy, b * CHUNKS + 2 * TC * i + n + 1)
                if 2 * TC * i + n >= TC:
                    dve.wait_ge(exp_rdy, b * CHUNKS + 2 * TC * i + n + 1 - TC)
                dve.nop(nofuse=True)
                shift = (TC - 1 - c) * P
                dve.tensor_tensor_reduce(neg[:, c, :], ps_s[n % 2][:],
                                         strips[:, 2 * i + n // TC, shift:shift + S],
                                         -1.0, BIG, ALU.add, ALU.min, nmax[:, n:n + 1]).then_inc(neg_rdy, 1)

            def reciprocal(b, m):
                n = m % (2 * TC)
                dve.wait_ge(exp_rdy, b * CHUNKS + m + 1)
                dve.reciprocal(rinv[:, n:n + 1], rsum[:, n:n + 1]).then_inc(rinv_rdy, 1)

            def weights_t(b, i, hh, j):
                dve.wait_ge(t_rdy, b * CHUNKS + 2 * TC * i + TC * hh + j + 1)
                dve.tensor_copy(probt[:, hh, j, :], ps_t[j % 2][:]).then_inc(pt_dve, 1)

            dve.wait_ge(ld_x0, 16)
            moments_of(0, 0)
            normalise(0, 0)
            for n in range(3):
                dve.wait_ge(w_hi_rdy, n + 1)
                dve.tensor_tensor(w_lo[n][:], stage[:], w_hi[n][:].bitcast(F32), ALU.subtract).then_inc(w_lo_rdy, 1)
            tokens_lo(0)
            for m in range(4):
                split_lo(0, 0, m)
            for h in range(H):
                dve.wait_ge(flip_rdy, 2 * h + 2)
                dve.tensor_copy(strips[:, h, STRIP // 2:STRIP], strip_bank[h % 2][1][:, 0:STRIP // 2]).then_inc(strip_dve, 1)
            dve.wait_ge(strip_act, H)
            dve.wait_ge(strip_dve, H)
            dve.wait_ge(ld_x, 16 * NB)
            with dve.Fori(0, NB) as b:
                for i in range(NPR):
                    for n in range(2 * TC):
                        m = 2 * TC * i + n
                        scores(b, i, n)
                        if m >= 2:
                            reciprocal(b, m - 2)
                        if n < TC and i:
                            weights_t(b, i - 1, n // 2, 2 * (n % 2))
                        if n >= TC and i + 1 < NPR:
                            split_lo(b, i + 1, n - TC)
                    if i == 3:
                        moments_of(b + 1, (b + 1) * TC)
                    if i == 5:
                        normalise(b + 1, (b + 1) * TC)
                reciprocal(b, CHUNKS - 2)
                tokens_lo(b + 1)
                reciprocal(b, CHUNKS - 1)
                weights_t(b, NPR - 1, 0, 0)
                weights_t(b, NPR - 1, 0, 2)
                for m in range(4):
                    split_lo(b + 1, 0, m)
                weights_t(b, NPR - 1, 1, 0)
                weights_t(b, NPR - 1, 1, 2)
                dve.wait_ge(o_rdy, (b + 1) * NPR)
                dve.tensor_tensor(x_all[:, bass.ds(b * TC, TC), :], ps_o[:].rearrange("p (c d) -> p c d", c=TC),
                                  x_all[:, bass.ds(b * TC, TC), :], ALU.add).then_inc(res_rdy, 1)

        @block.tensor
        def _(pe):
            def tokens_t(n):
                pe.wait_ge(xn_rdy, (n + 1) * TC)
                for c in range(TC):
                    mm = pe.transpose(ps_c[:, c * P:(c + 1) * P], xn[:, c, :], idn[:])
                mm.then_inc(xt_rdy, 1)

            def three(to, a_hi, a_lo, b_hi, b_lo):
                pe.matmul(to, a_lo, b_hi, start=True, stop=False)
                pe.matmul(to, a_hi, b_lo, start=False, stop=False)
                return pe.matmul(to, a_hi, b_hi, start=False, stop=True)

            def project(n, i, done):
                cols = slice(i * P, (i + 1) * P)
                three(ps_prj[(3 * i + n) % 2][:], w_hi[n][:, cols], w_lo[n][:, cols], xnt_hi[:], xnt_lo[:])\
                    .then_inc(done, 1)

            def project_v(b, i):
                pe.wait_ge(lo_rdy, b * HALVES + 4 * i + 2)
                cols = slice(i * P, (i + 1) * P)
                for c in range(TC):
                    tok = slice(c * P, (c + 1) * P)
                    mm = three(ps_prj[(3 * i + 2) % 2][:, tok], xnt_hi[:, tok], xnt_lo[:, tok],
                               w_hi[2][:, cols], w_lo[2][:, cols])
                mm.then_inc(v_rdy, 1)

            def scores(b, i, n):
                hh, c, m = n // TC, n % TC, 2 * TC * i + n
                if m >= 2:
                    pe.wait_ge(neg_rdy, b * CHUNKS + m - 1)
                if n == 0:
                    pe.wait_ge(lo_rdy, b * HALVES + 4 * (i + 1))
                    pe.wait_ge(ksw_rdy, b * (32 * NPR) + 32 * (i + 1))
                q = q_st[:, i % 2, hh, c * P:(c + 1) * P]
                pe.matmul(ps_s[n % 2][:], q, k_sw[:, i % 2, hh, :], start=True, stop=False)
                pe.matmul(ps_s[n % 2][:], q, k_st[:, i % 2, hh, :], start=False, stop=True).then_inc(s_rdy, 1)

            def weights_t(b, i, hh, j):
                m = 2 * TC * i + TC * hh + j
                if j == 0:
                    pe.wait_ge(norm_rdy, b * CHUNKS + 2 * TC * i + TC * (hh + 1))
                if m >= 2:
                    pe.wait_ge(pt_act if j % 2 else pt_dve, b * (CHUNKS // 2) + m // 2)
                for c in range(TC):
                    mm = pe.transpose(ps_t[j % 2][:, c * P:(c + 1) * P], prob[:, i % 2, hh, c, j * P:(j + 1) * P], idn[:])
                mm.then_inc(t_rdy, 1)

            def weigh(b, i, j):
                if j == 0:
                    pe.wait_ge(v_cp, b * NPR + i + 1)
                    if i >= 1:
                        pe.wait_ge(c_cp, b * NPR + i)
                pe.wait_ge(pt_act if j % 2 else pt_dve, b * (CHUNKS // 2) + TC * i + 2 + j // 2 + 1)
                for hh in range(2):
                    mm = pe.matmul(ps_c[DH * hh:DH * hh + DH, :], v_sb[:, i % 2, j, DH * hh:DH * hh + DH],
                                   probt[:, hh, j, :], start=(j == 0), stop=(j == TC - 1))
                if j == TC - 1:
                    mm.then_inc(c_rdy, 1)

            def project_out(b, i):
                pe.wait_ge(c_cp, b * NPR + i + 1)
                for c in range(TC):
                    mm = pe.matmul(ps_o[:, c * P:(c + 1) * P], ctxt[:, i % 2, c * P:(c + 1) * P], wo_sb[:, i, :],
                                   start=(i == 0 and c == 0), stop=(i == NPR - 1), skip_group_check=True)
                mm.then_inc(o_rdy, 1)

            pe.wait_ge(ld_c, 64)
            for a in range(2):
                pe.matmul(ps_s[a][0:H, :], rb_sb[:], onehot_sb[:, a, :], start=True, stop=True).then_inc(roll_mm, 1)
            tokens_t(0)
            pe.wait_ge(xlo_rdy, 1)
            for n, done in ((0, k_rdy), (1, q_rdy)):
                pe.wait_ge(w_lo_rdy, n + 1)
                project(n, 0, done)
            pe.wait_ge(w_lo_rdy, 3)
            project_v(0, 0)
            pe.wait_ge(ld_wo, 16)
            for h in range(H):
                g, a = h // TC, h % TC
                if a == 0:
                    pe.wait_ge(ld_strip[g], 16 * TC)
                for half in range(2):
                    if h >= 2:
                        pe.wait_ge(strip_dve if half else strip_act, h - 1)
                    pe.matmul(strip_bank[h % 2][half][:, 0:STRIP // 2], flip_sb,
                              raw_strips[:, g % 2, a * STRIP + half * (STRIP // 2):a * STRIP + (half + 1) * (STRIP // 2)],
                              start=True, stop=True).then_inc(flip_rdy, 1)
            pe.wait_ge(strip_act, H)
            pe.wait_ge(strip_dve, H)
            with pe.Fori(0, NB) as b:
                for i in range(NPR):
                    for c in range(TC):
                        scores(b, i, c)
                        if i:
                            weights_t(b, i - 1, c // 2, 2 * (c % 2))
                            weights_t(b, i - 1, c // 2, 2 * (c % 2) + 1)
                    if i + 1 < NPR:
                        project(0, i + 1, k_rdy)
                        pe.wait_ge(v_cp, b * NPR + i + 1)
                        project(1, i + 1, q_rdy)
                    for c in range(TC):
                        scores(b, i, TC + c)
                        if i:
                            weigh(b, i - 1, c)
                    if i + 1 < NPR:
                        project_v(b, i + 1)
                    if i >= 2:
                        project_out(b, i - 2)
                pe.wait_ge(c_cp, b * NPR + NPR - 1)
                tokens_t(b + 1)
                project_out(b, NPR - 2)
                for j in range(TC):
                    weights_t(b, NPR - 1, 0, j)
                pe.wait_ge(xlo_rdy, b + 2)
                pe.wait_ge(v_cp, b * NPR + NPR)
                project(0, 0, k_rdy)
                project(1, 0, q_rdy)
                for j in range(TC):
                    weights_t(b, NPR - 1, 1, j)
                project_v(b + 1, 0)
                for j in range(TC):
                    weigh(b, NPR - 1, j)
                project_out(b, NPR - 1)

        phase.close()
        attn.close()
        F = FC * P
        TOP = 4
        PIECE = 2048
        NPC = NE * F // PIECE
        xt = sb("xt", [P, S])
        xt_hi = sb("xt_hi", [P, T], F32R)
        xt_lo = sb("xt_lo", [P, T], F32R)
        w1_raw = sb("w1_raw", [P, 2, PIECE])
        w1_hi = sb("w1_hi", [P, NE * F], F32R)
        w1_lo = sb("w1_lo", [P, NE * F], F32R)
        w2_sb = sb("w2_sb", [P, NE * FC, D])
        b1_sb = sb("b1_sb", [P, NE * FC])
        b2_sb = sb("b2_sb", [NE, D])
        keys_sb = sb("keys_sb", [P, NE])
        rw_sb = sb("rw_sb", [P, NE])
        keys2 = sb("keys2", [P, NE])
        rk = sb("rk", [P, NE])
        lrow = sb("lrow", [1, NE])
        lconst = sb("lconst", [1, NE])
        ones = sb("ones", [P, P])
        eno = sb("eno", [P, NE])
        lg = sb("lg", [P, NCH, NE])
        top = sb("top", [P, NCH, 8])
        idx = sb("idx", [P, NCH, 8], U32)
        idxf = sb("idxf", [P, NCH, TOP])
        diff = sb("diff", [P, NCH, TOP])
        ev = sb("ev", [P, NCH, TOP])
        esum = sb("esum", [P, NCH])
        einv = sb("einv", [P, NCH])
        wt = sb("wt", [P, NCH, TOP])
        picked = sb("picked", [P, NCH, NE, TOP])
        gates = sb("gates", [P, NCH, NE])
        gcur = sb("gcur", [P, TC, NE])
        gt = sb("gt", [NE, S])
        ht = sb("ht", [P, 2, FC, S])

        ps_h, ps_y, ps_x, ps_l = [ps_s[0], ps_s[1], ps_t[0], ps_t[1]], ps_prj, ps_c, ps_o

        ld_r, ld_w1, ld_w2, one_rdy = sem("ld_r"), [sem("ld_w1_even"), sem("ld_w1_odd")], sem("ld_w2"), sem("one_rdy")
        w1hi_rdy, w1lo_rdy = sem("w1hi_rdy"), sem("w1lo_rdy")
        k2_rdy, kk_rdy, rk_rdy, lc_rdy = sem("k2_rdy"), sem("kk_rdy"), sem("rk_rdy"), sem("lc_rdy")
        st2, mv2, ve2, rstd2, xn2 = (sem(n) for n in ("st2", "mv2", "ve2", "rstd2", "xn2"))
        xt2_rdy, xcp_rdy, xhi2, xlo2 = sem("xt2_rdy"), sem("xcp_rdy"), sem("xhi2"), sem("xlo2")
        l_rdy, lg_rdy, top_rdy, idx_rdy, idxf_rdy, diff_rdy = (sem(n) for n in (
            "l_rdy", "lg_rdy", "top_rdy", "idx_rdy", "idxf_rdy", "diff_rdy"))
        ev_rdy, es_rdy, ei_rdy, wt_rdy, eq_rdy, pick_rdy, gate_rdy = (sem(n) for n in (
            "ev_rdy", "es_rdy", "ei_rdy", "wt_rdy", "eq_rdy", "pick_rdy", "gate_rdy"))
        gc_rdy, g_rdy, gt_rdy, b2_rdy, b2_add = (sem(n) for n in ("gc_rdy", "g_rdy", "gt_rdy", "b2_rdy", "b2_add"))
        h_rdy, gelu_rdy, y_rdy, acc_rdy = (sem(n) for n in ("h_rdy", "gelu_rdy", "y_rdy", "acc_rdy"))
        block = ctx.enter_context(nc.Block())

        @block.sync
        def _(sp):
            for to, src in ((keys_sb, keys_t), (rw_sb, rw_t), (lrow, rb), (eno, expert_no), (b1_sb, b1t), (b2_sb, b2)):
                sp.dma_start(to[:], src).then_inc(ld_r, 16)
            for n in range(NPC):
                if n >= 2:
                    sp.wait_ge(w1lo_rdy, n - 1)
                sp.dma_start(w1_raw[:, n % 2, :], w1t[:, n * PIECE:(n + 1) * PIECE]).then_inc(ld_w1[n % 2], 16)
            for n in range(NPC):
                c = NE * FC // NPC
                sp.dma_start(w2_sb[:, n * c:(n + 1) * c, :],
                             w2t[:, n * PIECE:(n + 1) * PIECE].rearrange("p (n d) -> p n d", d=D)).then_inc(ld_w2, 16)
            with sp.Fori(0, NB) as n:
                sp.wait_ge(acc_rdy, (n + 1) * (NE * TC))
                sp.dma_start(out[bass.ds(n * S, S), :].rearrange("(n p) d -> p n d", p=P),
                             x_all[:, bass.ds(n * TC, TC), :]).then_inc(st_out, 16)
            sp.wait_ge(st_out, 16 * NB)

        @block.gpsimd
        def _(pool):
            pool.memset(ones[:], 1.0).then_inc(one_rdy, 1)
            with pool.Fori(0, NB) as n:
                pool.wait_ge(ve2, n + 1)
                pool.tensor_tensor(rstd[:], var_eps[:], minus_half[:], ALU.pow).then_inc(rstd2, 1)

        @block.scalar
        def _(act):
            for n in range(NPC):
                act.wait_ge(ld_w1[n % 2], 16 * (n // 2 + 1))
                act.activation(w1_hi[:, n * PIECE:(n + 1) * PIECE], w1_raw[:, n % 2, :], ACT.Copy).then_inc(w1hi_rdy, 1)
            with act.Fori(0, NB) as n:
                act.wait_ge(xt2_rdy, n + 1)
                act.activation(xt[:], ps_x[:], ACT.Copy).then_inc(xcp_rdy, 1)
                act.activation(xt_hi[:, bass.ds(n * S, S)], ps_x[:], ACT.Copy).then_inc(xhi2, 1)
            act.wait_ge(diff_rdy, 1)
            act.activation(ev[:], diff[:], ACT.Exp).then_inc(ev_rdy, 1)
            act.wait_ge(ld_r, 96)
            with act.Fori(0, NB) as n:
                act.wait_ge(g_rdy, n + 1)
                act.activation(gt[:], ps_x[0:NE, :], ACT.Copy).then_inc(gt_rdy, 1)
                for e in range(NE):
                    for f in range(FC):
                        act.wait_ge(h_rdy, n * (NE * FC) + e * FC + f + 1)
                        if e >= 2 and f == 0:
                            act.wait_ge(y_rdy, n * NE + e - 1)
                        act.activation(ht[:, e % 2, f, :], ps_h[f][:], ACT.Gelu,
                                       bias=b1_sb[:, e * FC + f:e * FC + f + 1]).then_inc(gelu_rdy, 1)

        @block.vector
        def _(dve):
            dve.wait_ge(ld_r, 96)
            dve.tensor_tensor(keys2[:], keys_sb[:], keys_sb[:], ALU.mult).then_inc(k2_rdy, 1)
            dve.scalar_tensor_tensor(rk[:], keys_sb[:], 2.0, rw_sb[:], ALU.mult, ALU.add).then_inc(rk_rdy, 1)
            dve.wait_ge(kk_rdy, 1)
            dve.tensor_tensor(lconst[:], lrow[:], ps_l[0:1, 0:NE], ALU.subtract).then_inc(lc_rdy, 1)
            for n in range(NPC):
                dve.wait_ge(w1hi_rdy, n + 1)
                dve.tensor_tensor(w1_lo[:, n * PIECE:(n + 1) * PIECE], w1_raw[:, n % 2, :],
                                  w1_hi[:, n * PIECE:(n + 1) * PIECE].bitcast(F32), ALU.subtract).then_inc(w1lo_rdy, 1)
            with dve.Fori(0, NB) as n:
                for c in range(TC):
                    dve.bn_stats(stats[:, c, :], x_all[:, bass.ds(n * TC + c, 1), :]).then_inc(st2, 1)
                dve.wait_ge(st2, (n + 1) * TC)
                dve.nop(nofuse=True)
                for c in range(TC):
                    dve.bn_aggr(moments[:, c, :], stats[:, c, :]).then_inc(mv2, 1)
                dve.wait_ge(mv2, (n + 1) * TC)
                dve.tensor_scalar(var_eps[:], moments[:, :, 1], EPS, None, ALU.add).then_inc(ve2, 1)
                dve.wait_ge(rstd2, n + 1)
                for c in range(TC):
                    dve.tensor_scalar(xn[:, c, :], x_all[:, bass.ds(n * TC + c, 1), :], moments[:, c, 0:1],
                                      rstd[:, c:c + 1], ALU.subtract, ALU.mult).then_inc(xn2, 1)
                dve.wait_ge(xhi2, n + 1)
                dve.tensor_tensor(xt_lo[:, bass.ds(n * S, S)], ps_x[:], xt_hi[:, bass.ds(n * S, S)].bitcast(F32),
                                  ALU.subtract).then_inc(xlo2, 1)
                dve.wait_ge(l_rdy, n + 1)
                dve.tensor_copy(lg[:, bass.ds(n * TC, TC), :], ps_l[:, 0:TC * NE].rearrange("p (c e) -> p c e", e=NE))\
                    .then_inc(lg_rdy, 1)
            dve.wait_ge(lg_rdy, NB)
            for c in range(NCH):
                dve.max(top[:, c, :], lg[:, c, :]).then_inc(top_rdy, 1)
            for c in range(NCH):
                dve.wait_ge(top_rdy, c + 1)
                dve.max_index(idx[:, c, :], top[:, c, :], lg[:, c, :]).then_inc(idx_rdy, 1)
            dve.tensor_tensor(diff[:], top[:, :, 0:TOP], top[:, :, 0:1].broadcast_to([P, NCH, TOP]),
                              ALU.subtract).then_inc(diff_rdy, 1)
            dve.wait_ge(idx_rdy, NCH)
            dve.tensor_copy(idxf[:], idx[:, :, 0:TOP]).then_inc(idxf_rdy, 1)
            dve.wait_ge(ev_rdy, 1)
            dve.tensor_reduce(esum[:], ev[:], mybir.AxisListType.X, ALU.add).then_inc(es_rdy, 1)
            dve.wait_ge(es_rdy, 1)
            dve.reciprocal(einv[:], esum[:]).then_inc(ei_rdy, 1)
            dve.wait_ge(ei_rdy, 1)
            dve.tensor_tensor(wt[:], ev[:], einv[:].unsqueeze(2).broadcast_to([P, NCH, TOP]), ALU.mult).then_inc(wt_rdy, 1)
            dve.wait_ge(idxf_rdy, 1)
            for k in range(TOP):
                dve.tensor_tensor(picked[:, :, :, k], eno[:].unsqueeze(1).broadcast_to([P, NCH, NE]),
                                  idxf[:, :, k:k + 1].broadcast_to([P, NCH, NE]), ALU.is_equal).then_inc(eq_rdy, 1)
            dve.wait_ge(wt_rdy, 1)
            for k in range(TOP):
                dve.wait_ge(eq_rdy, k + 1)
                dve.tensor_tensor(picked[:, :, :, k], picked[:, :, :, k],
                                  wt[:, :, k:k + 1].broadcast_to([P, NCH, NE]), ALU.mult).then_inc(pick_rdy, 1)
            dve.wait_ge(pick_rdy, TOP)
            dve.tensor_reduce(gates[:], picked[:], mybir.AxisListType.X, ALU.add).then_inc(gate_rdy, 1)
            dve.wait_ge(gate_rdy, 1)
            with dve.Fori(0, NB) as n:
                dve.tensor_copy(gcur[:], gates[:, bass.ds(n * TC, TC), :]).then_inc(gc_rdy, 1)
                dve.wait_ge(b2_rdy, n + 1)
                here = x_all[:, bass.ds(n * TC, TC), :]
                dve.tensor_tensor(here, ps_l[:].rearrange("p (c d) -> p c d", c=TC), here, ALU.add).then_inc(b2_add, 1)
                for e in range(NE):
                    if e:
                        dve.wait_ge(acc_rdy, (n * NE + e) * TC)
                    else:
                        dve.wait_ge(b2_add, n + 1)
                    dve.wait_ge(y_rdy, n * NE + e + 1)
                    for c in range(TC):
                        acc = x_all[:, bass.ds(n * TC + c, 1), :]
                        dve.scalar_tensor_tensor(acc, ps_y[e % 2][:, c * D:(c + 1) * D].unsqueeze(1), gcur[:, c, e:e + 1], acc,
                                                 ALU.mult, ALU.add).then_inc(acc_rdy, 1)
                dve.wait_ge(acc_rdy, (n + 1) * (NE * TC))

        @block.tensor
        def _(pe):
            pe.wait_ge(one_rdy, 1)
            pe.wait_ge(k2_rdy, 1)
            pe.matmul(ps_l[0:1, 0:NE], ones[:, 0:1], keys2[:], start=True, stop=True).then_inc(kk_rdy, 1)
            pe.wait_ge(rk_rdy, 1)
            pe.wait_ge(lc_rdy, 1)
            with pe.Fori(0, NB) as n:
                pe.wait_ge(xn2, (n + 1) * TC)
                for c in range(TC):
                    mm = pe.transpose(ps_x[:, c * P:(c + 1) * P], xn[:, c, :], idn[:])
                mm.then_inc(xt2_rdy, 1)
                pe.wait_ge(xcp_rdy, n + 1)
                for c in range(TC):
                    to = ps_l[:, c * NE:(c + 1) * NE]
                    pe.matmul(to, xt[:, c * P:(c + 1) * P], rk[:], start=True, stop=False)
                    mm = pe.matmul(to, ones[0:1, :], lconst[:], start=False, stop=True)
                mm.then_inc(l_rdy, 1)
                pe.wait_ge(xlo2, n + 1)
                pe.wait_ge(lg_rdy, n + 1)
            pe.wait_ge(w1lo_rdy, NPC)
            pe.wait_ge(ld_w2, 16 * NPC)

            def second(n, e):
                pe.wait_ge(gelu_rdy, (n * NE + e + 1) * FC)
                if e >= 2:
                    pe.wait_ge(acc_rdy, (n * NE + e - 1) * TC)
                for c in range(TC):
                    for f in range(FC):
                        mm = pe.matmul(ps_y[e % 2][:, c * D:(c + 1) * D], ht[:, e % 2, f, c * P:(c + 1) * P],
                                       w2_sb[:, e * FC + f, :], start=(c == 0 and f == 0), stop=(f == FC - 1),
                                       skip_group_check=True)
                mm.then_inc(y_rdy, 1)

            with pe.Fori(0, NB) as n:
                pe.wait_ge(gc_rdy, n + 1)
                for c in range(TC):
                    mm = pe.transpose(ps_x[0:NE, c * P:(c + 1) * P], gcur[:, c, :], idn[:])
                mm.then_inc(g_rdy, 1)
                pe.wait_ge(gt_rdy, n + 1)
                for c in range(TC):
                    mm = pe.matmul(ps_l[:, c * D:(c + 1) * D], gt[:, c * P:(c + 1) * P], b2_sb[:], start=True, stop=True)
                mm.then_inc(b2_rdy, 1)
                hi, lo = (t[:, bass.ds(n * S, S)] for t in (xt_hi, xt_lo))
                for e in range(NE):
                    for f in range(FC):
                        if e:
                            pe.wait_ge(gelu_rdy, (n * NE + e - 1) * FC + f + 1)
                        cols = slice((e * FC + f) * P, (e * FC + f + 1) * P)
                        pe.matmul(ps_h[f][:], w1_lo[:, cols], hi, start=True, stop=False)
                        pe.matmul(ps_h[f][:], w1_hi[:, cols], lo, start=False, stop=False)
                        pe.matmul(ps_h[f][:], w1_hi[:, cols], hi, start=False, stop=True).then_inc(h_rdy, 1)
                    if e:
                        second(n, e - 1)
                second(n, NE - 1)
                pe.wait_ge(acc_rdy, (n + 1) * (NE * TC))


_INS = ["x", "wq", "wk", "wv", "wo", "rel_bias", "onehot", "ident", "flip", "expert_no", "w1t", "b1t", "w2t", "b2", "keys_t", "rw_t", "rb"]


def kernel(**inputs):
    import math

    import numpy as np
    import concourse.bacc as bacc
    from concourse.bass_utils import run_bass_kernel_spmd

    a = {k: np.asarray(v) for k, v in inputs.items()}
    hs = a["L0_attn_hidden_states"]
    B, S, D = hs.shape
    NBUCKET, H = a["L0_attn_rel_bias"].shape
    E, F, _ = a["L0_ffn_w1"].shape
    f32 = np.float32

    off = np.arange(-(S - 1), S + 1)
    half = NBUCKET // 2
    exact = half // 2
    dist = np.abs(off)
    far = exact + (np.log(np.maximum(dist, 1).astype(f32) / f32(exact)) / f32(math.log(128 / exact))
                   * f32(half - exact)).astype(np.int32)
    bucket = np.where(off > 0, half, 0) + np.where(dist < exact, dist, np.minimum(far, half - 1))
    onehot = (np.arange(NBUCKET)[:, None] == bucket[None, :]).astype(f32)

    arrays = {
        "x": hs.reshape(B * S, D),
        "wq": a["L0_attn_Wq"], "wk": a["L0_attn_Wk"], "wv": a["L0_attn_Wv"], "wo": a["L0_attn_Wo"],
        "rel_bias": a["L0_attn_rel_bias"], "onehot": onehot, "ident": np.eye(128, dtype=f32),
        "flip": np.ascontiguousarray(np.eye(128, dtype=f32)[::-1]),
        "expert_no": np.tile(np.arange(E, dtype=f32), (128, 1)),
        "w1t": a["L0_ffn_w1"].transpose(2, 0, 1).reshape(D, E * F),
        "b1t": a["L0_ffn_b1"].reshape(E * F // 128, 128).T,
        "w2t": a["L0_ffn_w2"].reshape(E, D, F // 128, 128).transpose(3, 0, 2, 1).reshape(128, -1),
        "b2": a["L0_ffn_b2"], "keys_t": a["L0_ffn_keys"].T, "rw_t": a["L0_ffn_rw"].T,
        "rb": a["L0_ffn_rb"].reshape(1, E),
    }
    arrays = {k: np.ascontiguousarray(v) for k, v in arrays.items()}
    nc = bacc.Bacc("TRN2", target_bir_lowering=False, num_devices=1)
    args = [nc.dram_tensor(f"in_{k}", arrays[k].shape, mybir.dt.from_np(arrays[k].dtype), kind="ExternalInput").ap()
            for k in _INS]
    res = nc.dram_tensor("out_0", (B * S, D), F32, kind="ExternalOutput").ap()
    layer_kernel(nc, *args, res)
    r = run_bass_kernel_spmd(nc, [{f"in_{k}": v for k, v in arrays.items()}], core_ids=[0])
    return r.results[0]["out_0"].reshape(B, S, D)
```

```python
from contextlib import ExitStack

import concourse.bass as bass
from concourse import mybir

F32 = mybir.dt.float32
F32R = mybir.dt.float32r
U32 = mybir.dt.uint32
I32 = mybir.dt.int32
ALU = mybir.AluOpType
ACT = mybir.ActivationFunctionType
AX = mybir.AxisListType

P = 128
DH = 64
TC = 4
TOP = 4
EPS = 1e-5
BIG = 3.0e38


def layer_kernel(nc, x, wq, wk, wv, wo, rel_bias, onehot, ident, flip, expert_no, before_tok, region, home_row, pad,
                 block_no, upto, w1t, w2t, biases, keys_t, rw_t, rb, out):
    T, D = x.shape
    S = TC * P
    NB = T // S
    LAST = NB - 1
    NCH = T // P
    H = wq.shape[1] // DH
    NPR = H // 2
    NE = rb.shape[1]
    F = w1t.shape[1] // NE
    FC = F // P
    NBUCKET = rel_bias.shape[0]
    ROLL = 2 * S
    STRIP = S + (TC - 1) * P
    NEAR = 3 * P
    FAR = (STRIP - NEAR) // 2
    VW = 2 * P
    TILES = 2 * TC
    CHUNKS = NPR * TILES
    PIECES = 4 * NPR
    REGION = T + P
    UN = 8
    NBLK = T * TOP // P + NE
    LAG = 3
    PIECE = 1024
    NPC = NE * F // PIECE
    CH_D = TC // 2
    SUM_D, SUM_P = TOP * CH_D, TOP
    YB = 4
    LD_R = 11 * 16

    with ExitStack() as ctx:
        def sb(name, shape, dt=F32, stack=ctx):
            return stack.enter_context(nc.sbuf_tensor(name, shape, dt))

        def sem(name):
            return ctx.enter_context(nc.semaphore(name))

        x_all = sb("x_all", [P, NCH, D])
        idn = sb("idn", [P, P])
        minus_half = sb("minus_half", [P, TC])
        stats = sb("stats", [P, 2, TC, 6])
        moments = sb("moments", [P, 2, TC, 2])
        var_eps = sb("var_eps", [P, 2, TC])
        rstd = sb("rstd", [P, 2, TC])
        xt = sb("xt", [P, S])
        keys_sb = sb("keys_sb", [P, NE])
        rw_sb = sb("rw_sb", [P, NE])
        keys2 = sb("keys2", [P, NE])
        rk = sb("rk", [P, NE])
        lrow = sb("lrow", [1, NE])
        lconst = sb("lconst", [1, NE])
        ones = sb("ones", [P, P])
        before_sb = sb("before_sb", [P, P])
        eno = sb("eno", [P, NE])
        region_sb = sb("region_sb", [P, NE])
        carry = sb("carry", [P, NE])
        home_sb = sb("home_sb", [P, NCH, TOP])
        pad_sb = sb("pad_sb", [P, D + 1])
        blkno_sb = sb("blkno_sb", [1, NBLK])
        upto_sb = sb("upto_sb", [1, NE, NE])
        lg = sb("lg", [P, TC, NE])
        top = sb("top", [P, TC, 8])
        idx = sb("idx", [P, TC, 8], U32)
        idxf = sb("idxf", [P, TC, TOP])
        diff = sb("diff", [P, TC, TOP])
        ev = sb("ev", [P, TC, TOP])
        esum = sb("esum", [P, TC])
        einv = sb("einv", [P, TC])
        wt = sb("wt", [P, NCH, TOP])
        picked = sb("picked", [P, TC, TOP, NE])
        mask = sb("mask", [P, TC, NE])
        free = sb("free", [P, TC, NE])
        slotf = sb("slotf", [P, TC, TOP])
        slot = sb("slot", [P, TC * TOP], I32)
        copies = sb("copies", [P, TC, 2, D + 1])

        strips_sb = sb("strips_sb", [P, H * STRIP])
        strips = strips_sb[:].rearrange("p (h m) -> p h m", h=H)
        BIAS_END = NE * (F + D)
        b_sb = strips_sb[:, 0:BIAS_END]
        w1_raw = strips_sb[:, BIAS_END:BIAS_END + 2 * PIECE].rearrange("p (a m) -> p a m", a=2)
        yb = strips_sb[:, BIAS_END + 2 * PIECE:BIAS_END + 2 * PIECE + UN * D].rearrange("p (n d) -> p n d", n=UN)

        attn = ctx.enter_context(ExitStack())
        xn = xt[:].rearrange("p (c d) -> p c d", c=TC)
        xnt_hi = sb("xnt_hi", [P, S], F32R, attn)
        xnt_lo = sb("xnt_lo", [P, S], F32R, attn)
        w_hi = [sb(f"w{n}_hi", [P, H * DH], F32R, attn)[:] for n in "kqv"]
        w_lo = [sb(f"w{n}_lo", [P, H * DH], F32R, attn)[:] for n in "kqv"]
        wo_sb = sb("wo_sb", [P, NPR, D], stack=attn)
        rb_sb = sb("rb_sb", [NBUCKET, H], stack=attn)
        q_st = sb("q_st", [P, 2, 2, S], F32R, attn)
        k_st = sb("k_st", [P, 2, 2, S], F32R, attn)
        k_sw = sb("k_sw", [P, 2, 2, S], F32R, attn)
        v_sb = sb("v_sb", [P, 2, TC, VW], stack=attn)
        neg = sb("neg", [P, 2, S], stack=attn)
        nmax = sb("nmax", [P, TILES], stack=attn)
        prob = sb("prob", [P, 2, 2, TC, S], stack=attn)
        rsum = sb("rsum", [P, TILES], stack=attn)
        rinv = sb("rinv", [P, TILES], stack=attn)
        probt = sb("probt", [P, 2, TC, S], stack=attn)
        ctxt = sb("ctxt", [P, 2, S], stack=attn)
        stage = [probt[:, 0, 2 * n:2 * n + 2, :].rearrange("p a m -> p (a m)") for n in range(2)] + \
                [probt[:, 1, 0:2, :].rearrange("p a m -> p (a m)")]
        scratch = prob[:].rearrange("p g h c s -> p (g h c s)")
        raw_strips = scratch[:, 0:H * NEAR].rearrange("p (h m) -> p h m", h=H)
        onehot_sb = scratch[0:NBUCKET, H * NEAR:H * NEAR + ROLL].rearrange("p (a m) -> p a m", a=2)
        roll_sb = scratch[0:H, H * NEAR + ROLL:H * NEAR + 2 * ROLL].rearrange("p (a m) -> p a m", a=2)
        flip_sb = neg[:, 0, 0:P]
        far_sb = neg[:, 1, 0:2 * H].rearrange("p (a h) -> p a h", a=2)

        roll_dram = nc.dram_tensor("roll_dram", [H, ROLL], F32, kind="Internal").ap()
        xs_dram = nc.dram_tensor("xs_dram", [NE * REGION + P, D + 1], F32, kind="Internal").ap()
        y_dram = nc.dram_tensor("y_dram", [TOP * T, D], F32, kind="Internal").ap()

        banks = [ctx.enter_context(nc.psum_tensor(f"bank{n}", [P, 512], F32)) for n in range(8)]
        ps_prj, ps_s, ps_t, ps_c, ps_o = banks[0:2], banks[2:4], banks[4:6], banks[6], banks[7]
        strip_bank = ps_s + ps_t

        ld_x0, ld_x, ld_c, ld_w = sem("ld_x0"), sem("ld_x"), sem("ld_c"), [sem(f"ld_w{n}") for n in "kqv"]
        ld_wo, roll_st, ld_strip = sem("ld_wo"), sem("roll_st"), [sem(f"ld_strip{g}") for g in range(H // TC)]
        ld_r, one_rdy = sem("ld_r"), sem("one_rdy")
        w_hi_rdy, w_lo_rdy = sem("w_hi_rdy"), sem("w_lo_rdy")
        roll_mm, roll_cp = sem("roll_mm"), sem("roll_cp")
        far_mm, far_cp, far_rdy = sem("far_mm"), sem("far_cp"), sem("far_rdy")
        flip_rdy, strip_act, strip_dve = sem("flip_rdy"), sem("strip_act"), sem("strip_dve")
        half_rdy = sem("half_rdy")
        st_rdy, mv_rdy, ve_rdy, rstd_rdy, xn_rdy = (sem(n) for n in ("st_rdy", "mv_rdy", "ve_rdy", "rstd_rdy", "xn_rdy"))
        xt_rdy, xhi_rdy, xlo_rdy = sem("xt_rdy"), sem("xhi_rdy"), sem("xlo_rdy")
        k_rdy, q_rdy, v_rdy = sem("k_rdy"), sem("q_rdy"), sem("v_rdy")
        hi_rdy, lo_rdy, v_cp = sem("hi_rdy"), sem("lo_rdy"), sem("v_cp")
        ksw_rdy = [sem("ksw_rdy0"), sem("ksw_rdy1")]
        s_rdy, neg_rdy, exp_rdy, rinv_rdy, norm_rdy = (sem(n) for n in
                                                       ("s_rdy", "neg_rdy", "exp_rdy", "rinv_rdy", "norm_rdy"))
        t_rdy, pt_act, pt_dve = sem("t_rdy"), sem("pt_act"), sem("pt_dve")
        c_rdy, c_cp, o_rdy, res_rdy = sem("c_rdy"), sem("c_cp"), sem("o_rdy"), sem("res_rdy")
        k2_rdy, kk_rdy, rk_rdy, lc_rdy = sem("k2_rdy"), sem("kk_rdy"), sem("rk_rdy"), sem("lc_rdy")
        st2, mv2, ve2, rstd2, xn2 = (sem(n) for n in ("st2", "mv2", "ve2", "rstd2", "xn2"))
        xt2_rdy, xcp_rdy, l_rdy, lg_rdy, top_rdy, idx_rdy = (sem(n) for n in (
            "xt2_rdy", "xcp_rdy", "l_rdy", "lg_rdy", "top_rdy", "idx_rdy"))
        diff_rdy, idxf_rdy, ev_rdy, es_rdy, ei_rdy, wt_rdy = (sem(n) for n in (
            "diff_rdy", "idxf_rdy", "ev_rdy", "es_rdy", "ei_rdy", "wt_rdy"))
        pick_rdy, mask_rdy, rank_rdy, free_rdy, carry_rdy, sel_rdy, slotf_rdy, slot_rdy = (sem(n) for n in (
            "pick_rdy", "mask_rdy", "rank_rdy", "free_rdy", "carry_rdy", "sel_rdy", "slotf_rdy", "slot_rdy"))
        copy_rdy, sent = sem("copy_rdy"), sem("sent")
        ld_w2, ld_b = sem("ld_w2"), sem("ld_b")

        def far_strips(a, first, end):
            return strips[:, first:end, a * (FAR + NEAR):a * (FAR + NEAR) + FAR]

        def far_bias(a, first, end):
            return far_sb[:, a, first:end].unsqueeze(2).broadcast_to([P, end - first, FAR])

        def bank_v(i):
            return ps_prj[(3 * i) % 2]

        def bank_kq(i, n):
            return ps_prj[(3 * i + 1 + n) % 2]

        def pair_piece(i, m):
            return bank_kq(i, m % 2), (k_st, q_st)[m % 2], m // 2

        def next_pair(b, i):
            return (b, i + 1) if i + 1 < NPR else (b + 1, 0)

        def before(b, i, k):
            return (b, i - k) if i >= k else (b - 1, i - k + NPR)

        def run_steps(eng, step, drain):
            for i in range(NPR):
                step(0, i)
            with eng.Fori(1, LAST) as b:
                for i in range(NPR):
                    step(b, i)
            for i in range(NPR):
                step(LAST, i)
            drain()

        def exists(b):
            return not (isinstance(b, int) and b < 0)

        def ends(b):
            return isinstance(b, int) and b == LAST

        def is_last(b, i):
            return ends(b) and i == NPR - 1

        def route_act(act, n, stage_no):
            if stage_no == 0:
                act.wait_ge(xt2_rdy, n + 1)
                act.activation(xt[:], ps_c[:], ACT.Copy).then_inc(xcp_rdy, 1)
            else:
                act.wait_ge(diff_rdy, n + 1)
                act.activation(ev[:], diff[:], ACT.Exp).then_inc(ev_rdy, 1)

        def route_pe(pe, n, stage_no):
            if stage_no == 0:
                pe.wait_ge(xn2, (n + 1) * TC)
                for c in range(TC):
                    mm = pe.transpose(ps_c[:, c * P:(c + 1) * P], copies[:, c, 0, 0:D], idn[:])
                mm.then_inc(xt2_rdy, 1)
            elif stage_no == 1:
                pe.wait_ge(xcp_rdy, n + 1)
                pe.matmul(ps_c[:, 0:TC * NE], ones[0:1, :], lconst[:].unsqueeze(1).broadcast_to([1, TC, NE]),
                          start=True, stop=False, skip_group_check=True)
                for c in range(TC):
                    mm = pe.matmul(ps_c[:, c * NE:(c + 1) * NE], xt[:, c * P:(c + 1) * P], rk[:],
                                   start=False, stop=True, skip_group_check=True)
                mm.then_inc(l_rdy, 1)
            else:
                pe.wait_ge(mask_rdy, n + 1)
                pe.matmul(ps_c[:, 0:TC * NE], before_sb[:], mask[:].rearrange("p c e -> p (c e)"),
                          start=True, stop=False, skip_group_check=True)
                for c in range(TC):
                    mm = pe.matmul(ps_c[:, (c + 1) * NE:(TC + 1) * NE], ones[:],
                                   mask[:, c:c + 1, :].broadcast_to([P, TC - c, NE]),
                                   start=False, stop=True, skip_group_check=True)
                mm.then_inc(rank_rdy, 1)

        SCATTERS = TC * TOP

        def route_pool(pool, n, stage_no):
            if stage_no == "rstd":
                pool.wait_ge(ve2, n + 1)
                pool.tensor_tensor(rstd[:, 1], var_eps[:, 1], minus_half[:], ALU.pow).then_inc(rstd2, 1)
            elif stage_no == "copy":
                pool.wait_ge(xn2, (n + 1) * TC)
                pool.nop(nofuse=True)
                pool.tensor_copy(copies[:, :, 1, 0:D], copies[:, :, 0, 0:D]).then_inc(copy_rdy, 1)
                pool.tensor_copy(copies[:, :, :, D], home_sb[:, bass.ds(n * TC, TC), 0:2]).then_inc(copy_rdy, 1)
            else:
                k, c = stage_no // TC, stage_no % TC
                if stage_no == 0:
                    pool.wait_ge(copy_rdy, n * 3 + 2)
                    pool.wait_ge(slot_rdy, n + 1)
                    pool.nop(nofuse=True)
                if stage_no == SCATTERS // 2:
                    pool.wait_ge(sent, n * (SCATTERS * 16) + SCATTERS // 2 * 16)
                    pool.nop(nofuse=True)
                    pool.tensor_copy(copies[:, :, :, D], home_sb[:, bass.ds(n * TC, TC), 2:4]).then_inc(copy_rdy, 1)
                    pool.wait_ge(copy_rdy, n * 3 + 3)
                    pool.nop(nofuse=True)
                pool.indirect_dma_start(xs_dram, bass.IndirectOffsetOnAxis(
                    ap=slot[:, c * TOP + k:c * TOP + k + 1], axis=0), copies[:, c, k % 2, :], None).then_inc(sent, 16)

        def moments_of(dve, n, q, stage_no, st, mv, ve):
            if stage_no == 0:
                for c in range(TC):
                    dve.bn_stats(stats[:, q, c, :], x_all[:, bass.ds(n * TC + c, 1), :]).then_inc(st, 1)
            elif stage_no == 1:
                dve.wait_ge(st, (n + 1) * TC)
                dve.nop(nofuse=True)
                for c in range(TC):
                    dve.bn_aggr(moments[:, q, c, :], stats[:, q, c, :]).then_inc(mv, 1)
            else:
                dve.wait_ge(mv, (n + 1) * TC)
                dve.tensor_scalar(var_eps[:, q], moments[:, q, :, 1], EPS, None, ALU.add).then_inc(ve, 1)

        def normalise(dve, n, q, to, ready, done):
            dve.wait_ge(ready, n + 1)
            for c in range(TC):
                dve.tensor_scalar(to[:, c, :], x_all[:, bass.ds(n * TC + c, 1), :], moments[:, q, c, 0:1],
                                  rstd[:, q, c:c + 1], ALU.subtract, ALU.mult).then_inc(done, 1)

        def route_dve(dve, n, stage_no):
            if stage_no < 3:
                moments_of(dve, n, 1, stage_no, st2, mv2, ve2)
            elif stage_no == 3:
                normalise(dve, n, 1, copies[:, :, 0, 0:D], rstd2, xn2)
            elif stage_no == 4:
                dve.wait_ge(l_rdy, n + 1)
                dve.tensor_copy(lg[:], ps_c[:, 0:TC * NE].rearrange("p (c e) -> p c e", e=NE)).then_inc(lg_rdy, 1)
            elif stage_no == 5:
                dve.wait_ge(lg_rdy, n + 1)
                dve.nop(nofuse=True)
                for c in range(TC):
                    dve.max(top[:, c, :], lg[:, c, :]).then_inc(top_rdy, 1)
            elif stage_no == 6:
                dve.wait_ge(top_rdy, (n + 1) * TC)
                dve.nop(nofuse=True)
                for c in range(TC):
                    dve.max_index(idx[:, c, :], top[:, c, :], lg[:, c, :]).then_inc(idx_rdy, 1)
                dve.tensor_tensor(diff[:], top[:, :, 0:TOP], top[:, :, 0:1].broadcast_to([P, TC, TOP]),
                                  ALU.subtract).then_inc(diff_rdy, 1)
            elif stage_no == 7:
                dve.wait_ge(idx_rdy, (n + 1) * TC)
                dve.tensor_copy(idxf[:], idx[:, :, 0:TOP]).then_inc(idxf_rdy, 1)
            elif stage_no == 8:
                dve.wait_ge(idxf_rdy, n + 1)
                dve.tensor_tensor(picked[:], eno[:].unsqueeze(1).unsqueeze(1).broadcast_to([P, TC, TOP, NE]),
                                  idxf[:].unsqueeze(3).broadcast_to([P, TC, TOP, NE]), ALU.is_equal).then_inc(pick_rdy, 1)
            elif stage_no == 9:
                dve.wait_ge(pick_rdy, n + 1)
                dve.tensor_reduce(mask[:], picked[:].rearrange("p c k e -> p c e k"), AX.X, ALU.add).then_inc(mask_rdy, 1)
            elif stage_no == 10:
                dve.wait_ge(ev_rdy, n + 1)
                dve.tensor_reduce(esum[:], ev[:], AX.X, ALU.add).then_inc(es_rdy, 1)
            elif stage_no == 11:
                dve.wait_ge(es_rdy, n + 1)
                dve.reciprocal(einv[:], esum[:]).then_inc(ei_rdy, 1)
            elif stage_no == 12:
                dve.wait_ge(ei_rdy, n + 1)
                dve.tensor_tensor(wt[:, bass.ds(n * TC, TC), :], ev[:], einv[:].unsqueeze(2).broadcast_to([P, TC, TOP]),
                                  ALU.mult).then_inc(wt_rdy, 1)
            elif stage_no == 13:
                dve.wait_ge(rank_rdy, n + 1)
                dve.tensor_tensor(free[:], ps_c[:, 0:TC * NE].rearrange("p (c e) -> p c e", e=NE),
                                  carry[:].unsqueeze(1).broadcast_to([P, TC, NE]), ALU.add).then_inc(free_rdy, 1)
            elif stage_no == 14:
                dve.wait_ge(free_rdy, n + 1)
                dve.tensor_tensor(carry[:], ps_c[:, TC * NE:(TC + 1) * NE], carry[:], ALU.add).then_inc(carry_rdy, 1)
                dve.wait_ge(mask_rdy, n + 1)
                dve.tensor_tensor(picked[:], picked[:], free[:].unsqueeze(2).broadcast_to([P, TC, TOP, NE]),
                                  ALU.mult).then_inc(sel_rdy, 1)
            elif stage_no == 15:
                dve.wait_ge(sel_rdy, n + 1)
                dve.tensor_reduce(slotf[:], picked[:], AX.X, ALU.add).then_inc(slotf_rdy, 1)
            else:
                dve.wait_ge(slotf_rdy, n + 1)
                dve.tensor_copy(slot[:], slotf[:].rearrange("p c k -> p (c k)")).then_inc(slot_rdy, 1)
                dve.wait_ge(carry_rdy, n + 1)

        ROUTE_STAGES = 17
        ROUTE_DVE = {(2, 2): 0, (2, 3): 1, (2, 5): 2, (3, 0): 3, (4, 2): 4, (4, 3): 5, (4, 4): 6, (4, 5): 7, (4, 6): 8,
                     (4, 7): 9, (5, 0): 10, (5, 1): 11, (5, 2): 13, (5, 3): 14, (5, 4): 12, (5, 5): 15, (5, 6): 16}
        ROUTE_PE = {(3, 2): 0, (4, 1): 1, (5, 1): 2}
        ROUTE_ACT = {(3, 3): 0, (4, 6): 1}
        ROUTE_POOL = {(2, 3): "rstd", (3, 1): "copy"}
        ROUTE_POOL.update({(5 + (4 + q) // TILES, (4 + q) % TILES): q for q in range(SCATTERS)})

        phase = ctx.enter_context(ExitStack())
        block = phase.enter_context(nc.Block())

        @block.sync
        def _(sp):
            sp.dma_start(rb_sb[:], rel_bias).then_inc(ld_c, 16)
            sp.dma_start(onehot_sb, onehot.rearrange("n (a m) -> n a m", a=2)).then_inc(ld_c, 16)
            sp.dma_start(x_all[:, 0:TC, :], x[0:S].rearrange("(n p) d -> p n d", p=P)).then_inc(ld_x0, 16)
            sp.dma_start(idn[:], ident).then_inc(ld_c, 16)
            sp.dma_start(flip_sb, flip).then_inc(ld_c, 16)
            for n, w in enumerate((wk, wq, wv)):
                sp.dma_start(stage[n], w).then_inc(ld_w[n], 16)
            sp.wait_ge(roll_cp, 2)
            sp.dma_start(roll_dram.rearrange("h (a m) -> h a m", a=2), roll_sb).then_inc(roll_st, 16)
            sp.wait_ge(roll_st, 16)
            for g in range(H // TC):
                sp.dma_start(raw_strips[:, g * TC:(g + 1) * TC, :],
                             bass.AP(roll_dram.tensor, g * TC * ROLL + FAR, [[1, P], [ROLL, TC], [1, NEAR]]))\
                    .then_inc(ld_strip[g], 16)
            for to, src in ((keys_sb, keys_t), (rw_sb, rw_t), (lrow, rb), (eno, expert_no), (before_sb, before_tok),
                            (region_sb, region), (carry, region), (home_sb, home_row.rearrange("p (n k) -> p n k", k=TOP)),
                            (pad_sb, pad), (blkno_sb, block_no),
                            (upto_sb, upto.rearrange("o (a b) -> o a b", a=NE))):
                sp.dma_start(to[:], src).then_inc(ld_r, 16)
            sp.dma_start(wo_sb[:], wo.rearrange("(n p) d -> p n d", p=P)).then_inc(ld_wo, 16)
            for n in range(1, NB):
                sp.dma_start(x_all[:, n * TC:(n + 1) * TC, :],
                             x[n * S:(n + 1) * S].rearrange("(n p) d -> p n d", p=P)).then_inc(ld_x, 16)
            with sp.Fori(0, NB) as b:
                for i in range(NPR):
                    for hh in range(2):
                        sp.wait_ge(lo_rdy, b * PIECES + 4 * i + 2 * hh + 1)
                        sp.dma_start(k_sw[0:DH, i % 2, hh].bitcast(F32), k_st[DH:P, i % 2, hh].bitcast(F32))\
                            .then_inc(ksw_rdy[hh], 16)
                        sp.dma_start(k_sw[DH:P, i % 2, hh].bitcast(F32), k_st[0:DH, i % 2, hh].bitcast(F32))\
                            .then_inc(ksw_rdy[hh], 16)
            sp.wait_ge(neg_rdy, LAST * CHUNKS + (BIAS_END // STRIP // 2 + 1) * TILES)
            for n in range(NE // 4):
                cols = slice(n * 4 * (F + D), (n + 1) * 4 * (F + D))
                sp.dma_start(b_sb[:, cols], biases[:, cols].broadcast_to([P, 4 * (F + D)])).then_inc(ld_b, 16)

        @block.gpsimd
        def _(pool):
            pool.memset(minus_half[:], -0.5).then_inc(half_rdy, 1)
            pool.memset(ones[:], 1.0).then_inc(one_rdy, 1)
            pool.wait_ge(half_rdy, 1)

            def rsqrt(n):
                pool.wait_ge(ve_rdy, n + 1)
                pool.tensor_tensor(rstd[:, 0], var_eps[:, 0], minus_half[:], ALU.pow).then_inc(rstd_rdy, 1)

            def step(b, i):
                for n in range(TILES):
                    if n % 2 == 0:
                        pool.wait_ge(rinv_rdy, b * (CHUNKS // 2) + (TILES * i + n) // 2 + 1)
                        pool.nop(nofuse=True)
                    tile = prob[:, i % 2, n // TC, n % TC, :]
                    pool.tensor_scalar(tile, tile, rinv[:, n:n + 1], 1.0, ALU.mult, ALU.mult).then_inc(norm_rdy, 1)
                    if i == 3 and n == 0 and not ends(b):
                        rsqrt(b + 1)
                    if (i, n) in ROUTE_POOL and exists(b - 1):
                        route_pool(pool, b - 1, ROUTE_POOL[i, n])
                if i == NPR - 1 and exists(b - 1):
                    pool.wait_ge(sent, b * (SCATTERS * 16))
                    pool.nop(nofuse=True)

            rsqrt(0)
            pool.wait_ge(far_cp, 1)
            for a in range(2):
                pool.tensor_copy(far_strips(a, H // 2, H), far_bias(a, H // 2, H)).then_inc(far_rdy, 1)
            pool.wait_ge(ld_r, LD_R)
            run_steps(pool, step, lambda: None)

        @block.scalar
        def _(act):
            def tokens_hi(n):
                act.wait_ge(xt_rdy, n + 1)
                act.activation(xnt_hi[:], ps_c[:], ACT.Copy).then_inc(xhi_rdy, 1)

            def split_hi(b, i, m):
                src, dst, hh = pair_piece(i, m)
                nb, ni = next_pair(b, i)
                act.wait_ge(q_rdy if m % 2 else k_rdy, nb * NPR + ni + 1)
                act.activation(dst[0:DH, ni % 2, hh, :], src[DH * hh:DH * hh + DH, :], ACT.Copy).then_inc(hi_rdy, 1)

            def values(b, i):
                act.wait_ge(v_rdy, b * NPR + i + 1)
                act.activation(v_sb[:, i // 2 % 2, 2 * (i % 2):2 * (i % 2) + 2, :].rearrange("p c d -> p (c d)"), bank_v(i)[:],
                               ACT.Copy).then_inc(v_cp, 1)

            def exps(b, i, n):
                act.wait_ge(neg_rdy, b * CHUNKS + TILES * i + n + 1)
                act.activation(prob[:, i % 2, n // TC, n % TC, :], neg[:, n % 2, :], ACT.Exp,
                               bias=nmax[:, n:n + 1], scale=-1.0, accum_out=rsum[:, n:n + 1]).then_inc(exp_rdy, 1)

            def weights_t(b, i, hh, j):
                act.wait_ge(t_rdy, b * CHUNKS + TILES * i + TC * hh + j + 1)
                act.activation(probt[:, hh, j, :], ps_t[j % 2][:], ACT.Copy).then_inc(pt_act, 1)

            def context(b, i):
                act.wait_ge(c_rdy, b * NPR + i + 1)
                act.activation(ctxt[:, i % 2, :], ps_c[:], ACT.Copy).then_inc(c_cp, 1)

            HI = {2: 0, 3: 1, 5: 2, 6: 3}
            HI_LATE = {4: 0, 5: 1, 6: 2, 7: 3}

            def step(b, i):
                hi = HI_LATE if i == NPR - 1 else HI
                for n in range(TILES):
                    if n == 0 and exists(before(b, i, 2)[0]):
                        context(*before(b, i, 2))
                    if 1 <= n <= TC and exists(before(b, i, 1)[0]):
                        weights_t(*before(b, i, 1), (n - 1) // 2, 2 * ((n - 1) % 2) + 1)
                    if n == 1:
                        values(b, i)
                    if n == 1 and i == NPR - 1 and not ends(b):
                        tokens_hi(b + 1)
                    if (i, n) in ROUTE_ACT and exists(b - 1):
                        route_act(act, b - 1, ROUTE_ACT[i, n])
                    if n in hi and not is_last(b, i):
                        split_hi(b, i, hi[n])
                    exps(b, i, n)

            def drain():
                context(LAST, NPR - 2)
                for hh in range(2):
                    weights_t(LAST, NPR - 1, hh, 1)
                    weights_t(LAST, NPR - 1, hh, 3)
                context(LAST, NPR - 1)

            for a in range(2):
                act.wait_ge(roll_mm, a + 1)
                act.activation(roll_sb[:, a, :], ps_s[a][0:H, :], ACT.Copy).then_inc(roll_cp, 1)
            act.wait_ge(far_mm, 1)
            act.activation(far_sb, ps_t[0][:, 0:2 * H].rearrange("p (a h) -> p a h", a=2), ACT.Copy).then_inc(far_cp, 1)
            for n in range(3):
                act.wait_ge(ld_w[n], 16)
                act.activation(w_hi[n], stage[n], ACT.Copy).then_inc(w_hi_rdy, 1)
                if n == 0:
                    tokens_hi(0)
            act.wait_ge(far_cp, 1)
            act.activation(far_strips(0, 0, H // 2), far_bias(0, 0, H // 2), ACT.Copy).then_inc(far_rdy, 1)
            for m in range(4):
                split_hi(-1, NPR - 1, m)
            for h in range(0, H, 2):
                act.wait_ge(flip_rdy, h + 1)
                act.activation(strips[:, h, FAR:FAR + NEAR], strip_bank[h % 4][:, 0:NEAR], ACT.Copy).then_inc(strip_act, 1)
            run_steps(act, step, drain)

        @block.vector
        def _(dve):
            def tokens_lo(n):
                dve.wait_ge(xhi_rdy, n + 1)
                dve.tensor_tensor(xnt_lo[:], ps_c[:], xnt_hi[:].bitcast(F32), ALU.subtract).then_inc(xlo_rdy, 1)

            def split_lo(b, i, m):
                src, dst, hh = pair_piece(i, m)
                nb, ni = next_pair(b, i)
                dve.wait_ge(hi_rdy, nb * PIECES + 4 * ni + m + 1)
                dve.tensor_tensor(dst[DH:P, ni % 2, hh, :], src[DH * hh:DH * hh + DH, :],
                                  dst[0:DH, ni % 2, hh, :].bitcast(F32), ALU.subtract).then_inc(lo_rdy, 1)

            def scores(b, i, n):
                m = TILES * i + n
                if not (isinstance(b, int) and b * CHUNKS + m < 2):
                    dve.wait_ge(exp_rdy, b * CHUNKS + m - 1)
                dve.wait_ge(s_rdy, b * CHUNKS + m + 1)
                dve.nop(nofuse=True)
                shift = (TC - 1 - n % TC) * P
                dve.tensor_tensor_reduce(neg[:, n % 2, :], ps_s[n % 2][:],
                                         strips[:, 2 * i + n // TC, shift:shift + S],
                                         -1.0, BIG, ALU.add, ALU.min, nmax[:, n:n + 1]).then_inc(neg_rdy, 1)

            def reciprocal(b, i, n):
                dve.wait_ge(exp_rdy, b * CHUNKS + TILES * i + n + 2)
                dve.reciprocal(rinv[:, n:n + 2], rsum[:, n:n + 2]).then_inc(rinv_rdy, 1)

            def weights_t(b, i, hh, j):
                dve.wait_ge(t_rdy, b * CHUNKS + TILES * i + TC * hh + j + 1)
                dve.tensor_copy(probt[:, hh, j, :], ps_t[j % 2][:]).then_inc(pt_dve, 1)

            def residual(b):
                dve.wait_ge(o_rdy, (b + 1) * NPR)
                dve.tensor_tensor(x_all[:, bass.ds(b * TC, TC), :], ps_o[:].rearrange("p (c d) -> p c d", c=TC),
                                  x_all[:, bass.ds(b * TC, TC), :], ALU.add).then_inc(res_rdy, 1)

            LO = {3: (0,), 4: (1,), 6: (2,), 7: (3,)}
            LO_LATE = {5: (0,), 6: (1,), 7: (2, 3)}
            NEXT = {(0, 5): 0, (1, 5): 1, (2, 4): 2}

            def step(b, i):
                lo = LO_LATE if i == NPR - 1 else LO
                for n in range(TILES):
                    scores(b, i, n)
                    if n == 0 and i == 2 and exists(b - 1):
                        residual(b - 1)
                    if n == 0 and exists(before(b, i, 1)[0]):
                        reciprocal(*before(b, i, 1), TILES - 2)
                    if n in (2, 4, 6):
                        reciprocal(b, i, n - 2)
                    if i == NPR - 2 and n == 5 and not ends(b):
                        normalise(dve, b + 1, 0, xn, rstd_rdy, xn_rdy)
                    if i == NPR - 1 and n == 2 and not ends(b):
                        tokens_lo(b + 1)
                    if (i, n) in NEXT and not ends(b):
                        moments_of(dve, b + 1, 0, NEXT[i, n], st_rdy, mv_rdy, ve_rdy)
                    if not is_last(b, i):
                        for m in lo.get(n, ()):
                            split_lo(b, i, m)
                    if n < TC and exists(before(b, i, 1)[0]):
                        weights_t(*before(b, i, 1), n // 2, 2 * (n % 2))
                    if (i, n) in ROUTE_DVE and exists(b - 1):
                        route_dve(dve, b - 1, ROUTE_DVE[i, n])

            def drain():
                reciprocal(LAST, NPR - 1, TILES - 2)
                for hh in range(2):
                    weights_t(LAST, NPR - 1, hh, 0)
                    weights_t(LAST, NPR - 1, hh, 2)
                residual(LAST)

            dve.wait_ge(ld_x0, 16)
            for stage_no in range(3):
                moments_of(dve, 0, 0, stage_no, st_rdy, mv_rdy, ve_rdy)
            normalise(dve, 0, 0, xn, rstd_rdy, xn_rdy)
            for n in range(3):
                dve.wait_ge(w_hi_rdy, n + 1)
                dve.tensor_tensor(w_lo[n], stage[n], w_hi[n].bitcast(F32), ALU.subtract).then_inc(w_lo_rdy, 1)
                if n == 0:
                    tokens_lo(0)
            dve.wait_ge(far_cp, 1)
            dve.tensor_copy(far_strips(1, 0, H // 2), far_bias(1, 0, H // 2)).then_inc(far_rdy, 1)
            for m in range(4):
                split_lo(-1, NPR - 1, m)
            for h in range(1, H, 2):
                dve.wait_ge(flip_rdy, h + 1)
                dve.tensor_copy(strips[:, h, FAR:FAR + NEAR], strip_bank[h % 4][:, 0:NEAR]).then_inc(strip_dve, 1)
            dve.wait_ge(ld_r, LD_R)
            dve.tensor_tensor(keys2[:], keys_sb[:], keys_sb[:], ALU.mult).then_inc(k2_rdy, 1)
            dve.scalar_tensor_tensor(rk[:], keys_sb[:], 2.0, rw_sb[:], ALU.mult, ALU.add).then_inc(rk_rdy, 1)
            dve.wait_ge(kk_rdy, 1)
            dve.tensor_tensor(lconst[:], lrow[:], ps_c[0:1, 0:NE], ALU.subtract).then_inc(lc_rdy, 1)
            dve.wait_ge(strip_act, H // 2)
            dve.wait_ge(strip_dve, H // 2)
            dve.wait_ge(far_rdy, 4)
            dve.wait_ge(ld_x, 16 * (NB - 1))
            run_steps(dve, step, drain)

        @block.tensor
        def _(pe):
            def tokens_t(n):
                pe.wait_ge(xn_rdy, (n + 1) * TC)
                for c in range(TC):
                    mm = pe.transpose(ps_c[:, c * P:(c + 1) * P], xn[:, c, :], idn[:])
                mm.then_inc(xt_rdy, 1)

            def three(to, a_hi, a_lo, b_hi, b_lo):
                pe.matmul(to, a_lo, b_hi, start=True, stop=False)
                pe.matmul(to, a_hi, b_lo, start=False, stop=False)
                return pe.matmul(to, a_hi, b_hi, start=False, stop=True)

            def project(i, n):
                ni = (i + 1) % NPR
                cols = slice(ni * P, (ni + 1) * P)
                three(bank_kq(i, n)[:], w_hi[n][:, cols], w_lo[n][:, cols], xnt_hi[:], xnt_lo[:])\
                    .then_inc((k_rdy, q_rdy)[n], 1)

            def project_v(i):
                cols = slice(i // 2 * VW, (i // 2 + 1) * VW)
                for a in range(2):
                    c = 2 * (i % 2) + a
                    tok = slice(c * P, (c + 1) * P)
                    mm = three(bank_v(i)[:, a * VW:(a + 1) * VW], xnt_hi[:, tok], xnt_lo[:, tok],
                               w_hi[2][:, cols], w_lo[2][:, cols])
                mm.then_inc(v_rdy, 1)

            def scores(b, i, n):
                m = TILES * i + n
                if not (isinstance(b, int) and b * CHUNKS + m < 2):
                    pe.wait_ge(neg_rdy, b * CHUNKS + m - 1)
                if n % TC == 0:
                    pe.wait_ge(lo_rdy, b * PIECES + 4 * i + 2 * (n // TC) + 2)
                    pe.wait_ge(ksw_rdy[n // TC], b * (32 * NPR) + 32 * (i + 1))
                q = q_st[:, i % 2, n // TC, (n % TC) * P:(n % TC + 1) * P]
                pe.matmul(ps_s[n % 2][:], q, k_st[:, i % 2, n // TC, :], start=True, stop=False)
                pe.matmul(ps_s[n % 2][:], q, k_sw[:, i % 2, n // TC, :], start=False, stop=True).then_inc(s_rdy, 1)

            def weights_t(b, i, hh, j):
                m = TILES * i + TC * hh + j
                if j == 0:
                    pe.wait_ge(norm_rdy, b * CHUNKS + TILES * i + TC * (hh + 1))
                if not (isinstance(b, int) and b * CHUNKS + m < 2):
                    pe.wait_ge(pt_act if j % 2 else pt_dve, b * (CHUNKS // 2) + m // 2)
                for c in range(TC):
                    mm = pe.transpose(ps_t[j % 2][:, c * P:(c + 1) * P], prob[:, i % 2, hh, c, j * P:(j + 1) * P], idn[:])
                mm.then_inc(t_rdy, 1)

            def weigh(b, i, j):
                if j == 0:
                    pe.wait_ge(v_cp, b * NPR + i - i % 2 + 2)
                    if not (isinstance(b, int) and b == 0 and i == 0):
                        pe.wait_ge(c_cp, b * NPR + i)
                pe.wait_ge(pt_act if j % 2 else pt_dve, b * (CHUNKS // 2) + TC * i + 2 + j // 2 + 1)
                for hh in range(2):
                    col = (i % 2) * P + DH * hh
                    mm = pe.matmul(ps_c[DH * hh:DH * hh + DH, :], v_sb[:, i // 2 % 2, j, col:col + DH],
                                   probt[:, hh, j, :], start=(j == 0), stop=(j == TC - 1))
                if j == TC - 1:
                    mm.then_inc(c_rdy, 1)

            def project_out(b, i, c):
                if c == 0:
                    pe.wait_ge(c_cp, b * NPR + i + 1)
                    if i == 0 and exists(b - 1):
                        pe.wait_ge(res_rdy, b)
                mm = pe.matmul(ps_o[:, c * P:(c + 1) * P], ctxt[:, i % 2, c * P:(c + 1) * P], wo_sb[:, i, :],
                               start=(i == 0 and c == 0), stop=(i == NPR - 1), skip_group_check=True)
                if c == TC - 1:
                    mm.then_inc(o_rdy, 1)

            def step(b, i):
                one, two = before(b, i, 1), before(b, i, 2)
                late = i == NPR - 1
                for n in range(TILES):
                    if n + 1 < TILES:
                        scores(b, i, n + 1)
                    elif not is_last(b, i):
                        scores(*next_pair(b, i), 0)
                    if n == 0:
                        pe.wait_ge(lo_rdy, b * PIECES + 4 * i + 3)
                        project_v(i)
                    if (i, n) in ROUTE_PE and exists(b - 1):
                        pe.wait_ge(c_cp, b * NPR + i - 1)
                        route_pe(pe, b - 1, ROUTE_PE[i, n])
                    if n == 1 and not late:
                        pe.wait_ge(lo_rdy, b * PIECES + 4 * i + 4)
                        project(i, 0)
                    if n < TC and exists(one[0]):
                        weights_t(*one, n // 2, 2 * (n % 2))
                        weights_t(*one, n // 2, 2 * (n % 2) + 1)
                    if n == 0 and late and not ends(b):
                        pe.wait_ge(c_cp, b * NPR + i - 1)
                        tokens_t(b + 1)
                    if n == 3 and late and not ends(b):
                        pe.wait_ge(lo_rdy, b * PIECES + 4 * i + 4)
                        pe.wait_ge(xlo_rdy, b + 2)
                        project(i, 0)
                    if n == (3 if late else 2) and not is_last(b, i):
                        pe.wait_ge(v_cp, b * NPR + i + 1)
                        project(i, 1)
                    if n == TC and exists(b - 1):
                        if i == 3:
                            pe.wait_ge(xcp_rdy, b)
                        if i == 4:
                            pe.wait_ge(lg_rdy, b)
                        if i == 5:
                            pe.wait_ge(carry_rdy, b)
                    if n >= TC and exists(one[0]):
                        weigh(*one, n - TC)
                    if n >= TC and exists(two[0]):
                        project_out(*two, n - TC)

            def drain():
                for c in range(TC):
                    project_out(LAST, NPR - 2, c)
                for hh in range(2):
                    for j in range(TC):
                        weights_t(LAST, NPR - 1, hh, j)
                for j in range(TC):
                    weigh(LAST, NPR - 1, j)
                for c in range(TC):
                    project_out(LAST, NPR - 1, c)

            pe.wait_ge(ld_c, 64)
            for a in range(2):
                pe.matmul(ps_s[a][0:H, :], rb_sb[:], onehot_sb[:, a, :], start=True, stop=True).then_inc(roll_mm, 1)
            for a, m in ((0, 0), (1, ROLL // 2 - 1)):
                mm = pe.matmul(ps_t[0][:, a * H:(a + 1) * H], onehot_sb[:, a, m:m + 1].broadcast_to([NBUCKET, P]), rb_sb[:],
                               start=True, stop=True)
            mm.then_inc(far_mm, 1)
            tokens_t(0)
            pe.wait_ge(xlo_rdy, 1)
            for n in range(2):
                pe.wait_ge(w_lo_rdy, n + 1)
                project(NPR - 1, n)
            pe.wait_ge(far_cp, 1)
            for h in range(H):
                if h % TC == 0:
                    pe.wait_ge(ld_strip[h // TC], 16)
                if h >= 4:
                    pe.wait_ge(strip_dve if h % 2 else strip_act, h // 2 - 1)
                pe.matmul(strip_bank[h % 4][:, 0:NEAR], flip_sb, raw_strips[:, h, :], start=True, stop=True)\
                    .then_inc(flip_rdy, 1)
            pe.wait_ge(one_rdy, 1)
            pe.wait_ge(k2_rdy, 1)
            pe.matmul(ps_c[0:1, 0:NE], ones[:, 0:1], keys2[:], start=True, stop=True).then_inc(kk_rdy, 1)
            pe.wait_ge(w_lo_rdy, 3)
            pe.wait_ge(ld_wo, 16)
            pe.wait_ge(rk_rdy, 1)
            pe.wait_ge(lc_rdy, 1)
            pe.wait_ge(strip_act, H // 2)
            pe.wait_ge(strip_dve, H // 2)
            scores(0, 0, 0)
            run_steps(pe, step, drain)

        phase.close()
        attn.close()
        w2_sb = sb("w2_sb", [P, NE * F])
        w1_hi = sb("w1_hi", [P, NE * F], F32R)
        w1_lo = sb("w1_lo", [P, NE * F], F32R)
        pad_at = sb("pad_at", [1, NE], I32)
        fill = sb("fill", [1, NE], I32)
        nblk_i = sb("nblk_i", [1, NE], I32)
        nblk = sb("nblk", [1, NE])
        cum = sb("cum", [1, NE, NE])
        ends = sb("ends", [1, NE])
        jump = sb("jump", [1, NE])
        eob = sb("eob", [1, NBLK])
        hops = sb("hops", [1, NBLK])
        rowf = sb("rowf", [1, NBLK])
        w_at = sb("w_at", [1, NBLK], I32)
        b_at = sb("b_at", [1, NBLK], I32)
        row_at = sb("row_at", [1, NBLK], I32)
        xb = sb("xb", [P, UN, D + 1])
        xbt_hi = sb("xbt_hi", [P, 2, P], F32R)
        xbt_lo = sb("xbt_lo", [P, 2, P], F32R)
        hidden_sb = sb("hidden_sb", [P, 3, 2, F])
        hb, act_h, act_t = hidden_sb[:, 0], hidden_sb[:, 1], hidden_sb[:, 2]
        home = sb("home", [P, UN], I32)
        yk = strips_sb[:, 0:YB * TOP * S].rearrange("p (a k c d) -> p a k c d", k=TOP, c=TC, d=D)
        past = hidden_sb[0:1].rearrange("p t a f -> p (t a f)")[:, 0:NBLK * NE].rearrange("p (n e) -> p n e", e=NE)

        ps_xt, ps_h, ps_g, ps_y = banks[0:2], banks[2:4], banks[4:6], banks[6:8]

        ld_w1, ld_pad = [sem("ld_w1_even"), sem("ld_w1_odd")], sem("ld_pad")
        w1hi_rdy, w1lo_rdy = sem("w1hi_rdy"), sem("w1lo_rdy")
        tab, at_rdy, pad_rdy, pads_sent = (sem(n) for n in ("tab", "at_rdy", "pad_rdy", "pads_sent"))
        ld_xb = [sem(f"ld_xb{j}") for j in range(UN)]
        xbt_rdy, xbhi_rdy, xblo_rdy, hh_rdy, hb_rdy = (sem(n) for n in ("xbt_rdy", "xbhi_rdy", "xblo_rdy", "hh_rdy", "hb_rdy"))
        gelu_rdy, gt_mm, gt_rdy, y_mm, home_rdy, yb_rdy = (sem(n) for n in (
            "gelu_rdy", "gt_mm", "gt_rdy", "y_mm", "home_rdy", "yb_rdy"))
        y_sent = [sem(f"y_sent{j}") for j in range(UN)]
        ld_y = [sem(f"ld_y{a}") for a in range(YB)]
        weighed, sum_d, sum_p = sem("weighed"), sem("sum_d"), sem("sum_p")
        st_out = sem("st_out")

        def starts(m, lag):
            return not isinstance(m, int) or m >= lag

        def run_blocks(eng, step, drain, regs=(), tables=()):
            def load(it):
                for r, t in zip(regs, tables):
                    for q in range(0, UN, 4):
                        eng.load(r[LAG + q:LAG + q + 4], t[0:1, bass.ds(it * UN + q, 4)])

            load(0)
            for j in range(UN):
                step(j, j)
            with eng.Fori(1, NBLK // UN) as it:
                for r in regs:
                    for j in range(LAG):
                        eng.reg_mov(r[j], r[UN + j])
                load(it)
                for j in range(UN):
                    step(it * UN + j, j)
            for r in regs:
                for j in range(LAG):
                    eng.reg_mov(r[j], r[UN + j])
            drain()

        block = ctx.enter_context(nc.Block())

        @block.sync
        def _(sp):
            def load_w1(n):
                if n >= 2:
                    sp.wait_ge(w1lo_rdy, n - 1)
                sp.dma_start(w1_raw[:, n % 2, :], w1t[:, n * PIECE:(n + 1) * PIECE]).then_inc(ld_w1[n % 2], 16)

            sp.dma_start(xs_dram[NE * REGION:NE * REGION + P, :], pad_sb[:]).then_inc(ld_pad, 16)
            def load_w2(n):
                cols = slice(n * PIECE, (n + 1) * PIECE)
                sp.dma_start(w2_sb[:, cols], w2t[:, cols]).then_inc(ld_w2, 16)

            load_w1(0)
            load_w1(1)
            for n in range(4):
                load_w2(n)
            for n in range(2, NPC - 2):
                load_w1(n)
                load_w2(n + 2)
            ends_at = [sp.alloc_register(f"end{e}") for e in range(4)]
            sp.wait_ge(pad_rdy, 1)
            for e in range(NE):
                if e % 4 == 0:
                    sp.load(ends_at, pad_at[0:1, e:e + 4])
                end = sp.snap(ends_at[e % 4], min_val=0, max_val=NE * REGION - P)
                sp.dma_start(xs_dram[bass.ds(end, P), :], pad_sb[:]).then_inc(pads_sent, 16)
            for n in range(NPC - 2, NPC):
                load_w1(n)

            rows = [sp.alloc_register(f"row{j}") for j in range(LAG + UN)]

            def step(m, j):
                if not isinstance(m, int):
                    sp.wait_ge(xbt_rdy, m - UN + 1)
                    sp.wait_ge(home_rdy, m - UN + 1)
                row = sp.snap(rows[LAG + j], min_val=0, max_val=NE * REGION)
                sp.dma_start(xb[:, j, :], xs_dram[bass.ds(row, P), :]).then_inc(ld_xb[j], 16)

            sp.wait_ge(ld_pad, 16)
            sp.wait_ge(at_rdy, 3)
            sp.wait_ge(sent, NB * SCATTERS * 16)
            sp.wait_ge(pads_sent, NE * 16)
            run_blocks(sp, step, lambda: None, [rows], [row_at])
            for j in range(UN):
                sp.wait_ge(y_sent[j], 16 * (NBLK // UN))

            def fetch(n):
                for k in range(TOP):
                    sp.dma_start(yk[:, n % YB, k], y_dram[k * T + n * S:k * T + (n + 1) * S, :]
                                 .rearrange("(c p) d -> p c d", p=P)).then_inc(ld_y[n % YB], 16)

            for n in range(YB):
                fetch(n)
            for n in range(NB):
                sp.wait_ge(sum_d, (n + 1) * SUM_D)
                sp.wait_ge(sum_p, (n + 1) * SUM_P)
                sp.dma_start(out[n * S:(n + 1) * S, :].rearrange("(n p) d -> p n d", p=P),
                             x_all[:, n * TC:(n + 1) * TC, :]).then_inc(st_out, 16)
                if n + YB < NB:
                    fetch(n + YB)
            sp.wait_ge(st_out, 16 * NB)

        @block.gpsimd
        def _(pool):
            route_pool(pool, LAST, "rstd")
            route_pool(pool, LAST, "copy")
            for q in range(SCATTERS):
                route_pool(pool, LAST, q)
            def step(m, j):
                pool.wait_ge(home_rdy, m + 1)
                pool.wait_ge(yb_rdy, m + 1)
                pool.nop(nofuse=True)
                pool.indirect_dma_start(y_dram, bass.IndirectOffsetOnAxis(ap=home[:, j:j + 1], axis=0), yb[:, j, :], None,
                                        bounds_check=TOP * T - 1, oob_is_err=False).then_inc(y_sent[j], 16)

            run_blocks(pool, step, lambda: None)
            for n in range(NB):
                here = x_all[:, n * TC + CH_D:(n + 1) * TC, :]
                for k in range(TOP):
                    pool.wait_ge(weighed, (n * TOP + k + 1) * (TC - CH_D))
                    if k:
                        pool.wait_ge(sum_p, n * SUM_P + k)
                    pool.tensor_tensor(here, here, yk[:, n % YB, k, CH_D:TC, :], ALU.add).then_inc(sum_p, 1)

        @block.scalar
        def _(act):
            def split_hi(n):
                act.wait_ge(ld_w1[n % 2], 16 * (n // 2 + 1))
                act.activation(w1_hi[:, n * PIECE:(n + 1) * PIECE], w1_raw[:, n % 2, :], ACT.Copy).then_inc(w1hi_rdy, 1)

            route_act(act, LAST, 0)
            split_hi(0)
            split_hi(1)
            route_act(act, LAST, 1)
            for n in range(2, NPC):
                split_hi(n)

            def turned_hi(m, q):
                act.wait_ge(xbt_rdy, m + 1)
                act.activation(xbt_hi[:, q % 2, :], ps_xt[q % 2][:, 0:P], ACT.Copy).then_inc(xbhi_rdy, 1)

            def hidden_t(m, q):
                act.wait_ge(gt_mm, m + 1)
                act.activation(act_t[:, q % 2, :], ps_g[q % 2][:], ACT.Copy).then_inc(gt_rdy, 1)

            def gelu(m, q):
                act.wait_ge(hb_rdy, m + 1)
                act.activation(act_h[:, q % 2, :], hb[:, q % 2, :], ACT.Gelu).then_inc(gelu_rdy, 1)

            def step(m, j):
                turned_hi(m, j)
                if starts(m, 2):
                    hidden_t(m - 2, j - 2)
                if starts(m, 1):
                    gelu(m - 1, j - 1)

            def drain():
                hidden_t(NBLK - 2, -2)
                gelu(NBLK - 1, -1)
                hidden_t(NBLK - 1, -1)

            run_blocks(act, step, drain)
            for n in range(NB):
                act.wait_ge(ld_y[n % YB], 16 * TOP * (n // YB + 1))
                for k in range(TOP):
                    for c in range(CH_D, TC):
                        rows = yk[:, n % YB, k, c, :]
                        act.activation(rows, rows, ACT.Copy, scale=wt[:, n * TC + c, k:k + 1]).then_inc(weighed, 1)

        @block.vector
        def _(dve):
            def split_lo(n):
                dve.wait_ge(w1hi_rdy, n + 1)
                dve.tensor_tensor(w1_lo[:, n * PIECE:(n + 1) * PIECE], w1_raw[:, n % 2, :],
                                  w1_hi[:, n * PIECE:(n + 1) * PIECE].bitcast(F32), ALU.subtract).then_inc(w1lo_rdy, 1)

            for stage_no in range(ROUTE_STAGES):
                route_dve(dve, LAST, stage_no)
                if stage_no == 3:
                    split_lo(0)
                    split_lo(1)
            dve.tensor_copy(pad_at[:], carry[0:1, :]).then_inc(pad_rdy, 1)
            for n in range(2, NPC - 2):
                split_lo(n)
            dve.scalar_tensor_tensor(fill[:], carry[0:1, :], float(P - 1), region_sb[0:1, :], ALU.add, ALU.subtract)\
                .then_inc(tab, 1)
            dve.wait_ge(tab, 1)
            dve.tensor_scalar(nblk_i[:], fill[:], P.bit_length() - 1, None, ALU.logical_shift_right).then_inc(tab, 1)
            dve.wait_ge(tab, 2)
            dve.tensor_copy(nblk[:], nblk_i[:]).then_inc(tab, 1)
            dve.wait_ge(tab, 3)
            dve.tensor_tensor(cum[:], upto_sb[:], nblk[:].unsqueeze(1).broadcast_to([1, NE, NE]), ALU.mult).then_inc(tab, 1)
            dve.tensor_scalar(jump[:], nblk[:], float(-P), float(REGION), ALU.mult, ALU.add).then_inc(tab, 1)
            dve.wait_ge(tab, 5)
            dve.tensor_reduce(ends[:], cum[:], AX.X, ALU.add).then_inc(tab, 1)
            dve.wait_ge(tab, 6)
            dve.tensor_tensor(past, blkno_sb[:].unsqueeze(2).broadcast_to([1, NBLK, NE]),
                              ends[:].unsqueeze(1).broadcast_to([1, NBLK, NE]), ALU.is_ge).then_inc(tab, 1)
            dve.wait_ge(tab, 7)
            dve.tensor_reduce(eob[:], past, AX.X, ALU.add).then_inc(tab, 1)
            dve.wait_ge(tab, 8)
            dve.tensor_tensor(past, past, jump[:].unsqueeze(1).broadcast_to([1, NBLK, NE]), ALU.mult).then_inc(tab, 1)
            dve.wait_ge(tab, 9)
            dve.tensor_reduce(hops[:], past, AX.X, ALU.add).then_inc(tab, 1)
            dve.tensor_scalar(w_at[:], eob[:], float(NE - 1), float(F), ALU.min, ALU.mult).then_inc(at_rdy, 1)
            dve.tensor_scalar(b_at[:], eob[:], float(NE - 1), float(F + D), ALU.min, ALU.mult).then_inc(at_rdy, 1)
            dve.wait_ge(tab, 10)
            dve.scalar_tensor_tensor(rowf[:], blkno_sb[:], float(P), hops[:], ALU.mult, ALU.add).then_inc(tab, 1)
            dve.wait_ge(tab, 11)
            dve.tensor_scalar(row_at[:], rowf[:], float(NE * REGION), None, ALU.min).then_inc(at_rdy, 1)

            for n in range(NPC - 2, NPC):
                split_lo(n)

            at = [dve.alloc_register(f"b_at{j}") for j in range(LAG + UN)]

            def turned_lo(m, q):
                dve.wait_ge(xbhi_rdy, m + 1)
                dve.tensor_tensor(xbt_lo[:, q % 2, :], ps_xt[q % 2][:, 0:P], xbt_hi[:, q % 2, :].bitcast(F32),
                                  ALU.subtract).then_inc(xblo_rdy, 1)

            def add_b1(m, q):
                b = dve.snap(at[LAG + q], min_val=0, max_val=(NE - 1) * (F + D))
                dve.wait_ge(hh_rdy, m + 1)
                dve.tensor_tensor(hb[:, q % 2, :], ps_h[q % 2][:], b_sb[:, bass.ds(b, F)], ALU.add).then_inc(hb_rdy, 1)

            def finish(m, q):
                j = q % UN
                b = dve.snap(at[LAG + q], min_val=0, max_val=(NE - 1) * (F + D))
                dve.wait_ge(ld_xb[j], 16 * ((m - j) // UN + 1) if isinstance(m, int) else (m - j) * (16 // UN) + 16)
                dve.tensor_copy(home[:, j:j + 1], xb[:, j, D:D + 1]).then_inc(home_rdy, 1)
                dve.wait_ge(y_mm, m + 1)
                dve.tensor_tensor(yb[:, j, :], ps_y[q % 2][:, 0:D], b_sb[:, bass.ds(b + F, D)], ALU.add).then_inc(yb_rdy, 1)

            def step(m, j):
                if not isinstance(m, int):
                    dve.wait_ge(y_sent[j], (m - j) * (16 // UN))
                turned_lo(m, j)
                if starts(m, 1):
                    add_b1(m - 1, j - 1)
                if starts(m, LAG):
                    finish(m - LAG, j - LAG)

            def drain():
                finish(NBLK - 3, -3)
                add_b1(NBLK - 1, -1)
                finish(NBLK - 2, -2)
                finish(NBLK - 1, -1)

            dve.wait_ge(at_rdy, 3)
            dve.wait_ge(ld_b, 16 * (NE // 4))
            run_blocks(dve, step, drain, [at], [b_at])
            for n in range(NB):
                dve.wait_ge(ld_y[n % YB], 16 * TOP * (n // YB + 1))
                for k in range(TOP):
                    for c in range(CH_D):
                        if k:
                            dve.wait_ge(sum_d, n * SUM_D + (k - 1) * CH_D + c + 1)
                        here = x_all[:, n * TC + c, :]
                        dve.scalar_tensor_tensor(here, yk[:, n % YB, k, c, :], wt[:, n * TC + c, k:k + 1], here,
                                                 ALU.mult, ALU.add).then_inc(sum_d, 1)

        @block.tensor
        def _(pe):
            for stage_no in range(3):
                route_pe(pe, LAST, stage_no)
                if stage_no == 1:
                    pe.wait_ge(lg_rdy, NB)
            pe.wait_ge(w1lo_rdy, NPC)
            pe.wait_ge(ld_w2, 16 * NPC)
            pe.wait_ge(at_rdy, 3)

            at = [pe.alloc_register(f"w_at{j}") for j in range(LAG + UN)]

            def weights_at(q):
                return pe.snap(at[LAG + q], min_val=0, max_val=(NE - 1) * F)

            def turn(m, q):
                j = q % UN
                if not isinstance(m, int) or m >= 2:
                    pe.wait_ge(xblo_rdy, m - 1)
                pe.wait_ge(ld_xb[j], 16 * (m // UN + 1) if isinstance(m, int) else (m - j) * (16 // UN) + 16)
                pe.transpose(ps_xt[q % 2][:, 0:P], xb[:, j, 0:D], idn[:]).then_inc(xbt_rdy, 1)

            def hidden(m, q):
                at = weights_at(q)
                if not isinstance(m, int) or m >= 2:
                    pe.wait_ge(hb_rdy, m - 1)
                pe.wait_ge(xblo_rdy, m + 1)
                hi, lo = xbt_hi[:, q % 2, :], xbt_lo[:, q % 2, :]
                pe.matmul(ps_h[q % 2][:], hi, w1_lo[:, bass.ds(at, F)], start=True, stop=False)
                pe.matmul(ps_h[q % 2][:], hi, w1_hi[:, bass.ds(at, F)], start=False, stop=False)
                pe.matmul(ps_h[q % 2][:], lo, w1_hi[:, bass.ds(at, F)], start=False, stop=True).then_inc(hh_rdy, 1)

            def hidden_t(m, q):
                if not isinstance(m, int) or m >= 2:
                    pe.wait_ge(gt_rdy, m - 1)
                pe.wait_ge(gelu_rdy, m + 1)
                for f in range(FC):
                    mm = pe.transpose(ps_g[q % 2][:, f * P:(f + 1) * P], act_h[:, q % 2, f * P:(f + 1) * P], idn[:])
                mm.then_inc(gt_mm, 1)

            def second(m, q):
                at = weights_at(q)
                if not isinstance(m, int) or m >= 2:
                    pe.wait_ge(yb_rdy, m - 1)
                pe.wait_ge(gt_rdy, m + 1)
                for f in range(FC):
                    mm = pe.matmul(ps_y[q % 2][:, 0:D], act_t[:, q % 2, f * P:(f + 1) * P],
                                   w2_sb[:, bass.ds(at + f * P, P)], start=(f == 0), stop=(f == FC - 1))
                mm.then_inc(y_mm, 1)

            def step(m, j):
                turn(m, j)
                if starts(m, 1):
                    hidden(m - 1, j - 1)
                if starts(m, 2):
                    hidden_t(m - 2, j - 2)
                if starts(m, LAG):
                    second(m - LAG, j - LAG)

            def drain():
                hidden(NBLK - 1, -1)
                hidden_t(NBLK - 2, -2)
                second(NBLK - 3, -3)
                hidden_t(NBLK - 1, -1)
                second(NBLK - 2, -2)
                second(NBLK - 1, -1)

            run_blocks(pe, step, drain, [at], [w_at])


_INS = ["x", "wq", "wk", "wv", "wo", "rel_bias", "onehot", "ident", "flip", "expert_no", "before_tok", "region", "home_row", "pad",
         "block_no", "upto", "w1t", "w2t", "biases", "keys_t", "rw_t", "rb"]


def kernel(**inputs):
    import math

    import numpy as np
    import concourse.bacc as bacc
    from concourse.bass_utils import run_bass_kernel_spmd

    a = {k: np.asarray(v) for k, v in inputs.items()}
    hs = a["L0_attn_hidden_states"]
    B, S, D = hs.shape
    NBUCKET, H = a["L0_attn_rel_bias"].shape
    E, F, _ = a["L0_ffn_w1"].shape
    f32 = np.float32

    off = np.arange(-(S - 1), S + 1)
    half = NBUCKET // 2
    exact = half // 2
    dist = np.abs(off)
    far = exact + (np.log(np.maximum(dist, 1).astype(f32) / f32(exact)) / f32(math.log(128 / exact))
                   * f32(half - exact)).astype(np.int32)
    bucket = np.where(off > 0, half, 0) + np.where(dist < exact, dist, np.minimum(far, half - 1))
    onehot = (np.arange(NBUCKET)[:, None] == bucket[None, :]).astype(f32)

    tok = np.arange(128, dtype=f32)
    home_row = (tok[:, None, None] + 128 * np.arange(B * S // 128, dtype=f32)[:, None]
                + B * S * np.arange(4, dtype=f32)).reshape(128, -1)
    pad = np.zeros((128, D + 1), f32)
    pad[:, D] = 4 * B * S

    arrays = {
        "x": hs.reshape(B * S, D),
        "wq": a["L0_attn_Wq"], "wk": a["L0_attn_Wk"], "wv": a["L0_attn_Wv"], "wo": a["L0_attn_Wo"],
        "rel_bias": a["L0_attn_rel_bias"], "onehot": onehot, "ident": np.eye(128, dtype=f32),
        "flip": np.ascontiguousarray(np.eye(128, dtype=f32)[::-1]),
        "expert_no": np.tile(np.arange(E, dtype=f32), (128, 1)),
        "before_tok": np.triu(np.ones((128, 128), f32), 1), "region": np.tile(np.arange(E, dtype=f32) * (B * S + 128), (128, 1)),
        "home_row": home_row, "pad": pad, "block_no": np.arange(B * S * 4 // 128 + E, dtype=f32)[None],
        "upto": np.tril(np.ones((E, E), f32)).reshape(1, -1),
        "w1t": a["L0_ffn_w1"].transpose(2, 0, 1).reshape(D, E * F),
        "w2t": a["L0_ffn_w2"].reshape(E, D, F // 128, 128).transpose(3, 0, 2, 1).reshape(128, -1),
        "biases": np.concatenate([a["L0_ffn_b1"], a["L0_ffn_b2"]], axis=1).reshape(1, -1),
        "keys_t": a["L0_ffn_keys"].T, "rw_t": a["L0_ffn_rw"].T,
        "rb": a["L0_ffn_rb"].reshape(1, E),
    }
    arrays = {k: np.ascontiguousarray(v) for k, v in arrays.items()}
    nc = bacc.Bacc("TRN2", target_bir_lowering=False, num_devices=1)
    args = [nc.dram_tensor(f"in_{k}", arrays[k].shape, mybir.dt.from_np(arrays[k].dtype), kind="ExternalInput").ap()
            for k in _INS]
    res = nc.dram_tensor("out_0", (B * S, D), F32, kind="ExternalOutput").ap()
    layer_kernel(nc, *args, res)
    r = run_bass_kernel_spmd(nc, [{f"in_{k}": v for k, v in arrays.items()}], core_ids=[0])
    return r.results[0]["out_0"].reshape(B, S, D)
```

```python
from contextlib import ExitStack

import concourse.bass as bass
from concourse import mybir

F32 = mybir.dt.float32
F32R = mybir.dt.float32r
BF16 = mybir.dt.bfloat16
U32 = mybir.dt.uint32
I32 = mybir.dt.int32
ALU = mybir.AluOpType
ACT = mybir.ActivationFunctionType
AX = mybir.AxisListType

P = 128
DH = 64
TC = 4
TOP = 4
EPS = 1e-5
BIG = 3.0e38


def layer_kernel(nc, x, wq, wk, wv, wo, rel_bias, onehot, ident, expert_no, before_tok, region, home_row, pad,
                 block_no, upto, seg_row, par_step, experts, b2, keys_t, rw_t, rb, out):
    T, D = x.shape
    S = TC * P
    NB = T // S
    LAST = NB - 1
    NCH = T // P
    H = wq.shape[1] // DH
    NPR = H // 2
    NE = rb.shape[1]
    F = experts.shape[2] * P // (P + D + 1)
    FC = F // P
    NBUCKET = rel_bias.shape[0]
    ROLL = 2 * S
    STRIP = S + (TC - 1) * P
    NEAR = 3 * P
    FAR = (STRIP - NEAR) // 2
    VW = 2 * P
    TILES = 2 * TC
    CHUNKS = NPR * TILES
    PIECES = 4 * NPR
    BC = 2
    BLK = BC * P
    REGION = T + BLK
    UN = 8
    NBLK = (T * TOP + NE * (BLK - 1)) // BLK
    NTAB = -(-NBLK // UN) * UN
    REST = (NBLK - 1) // UN
    END = NBLK - REST * UN
    NSEG = 2 * NE
    EARLY = 4 * UN
    assert EARLY <= ((T - S) * TOP - NE * (BLK - 1)) // BLK
    PEEL = 2 * UN
    LAG = 2
    BCH = 512 // BLK
    W2, B1, B2 = F, 2 * F, 2 * F + FC
    EW = B2 + D
    CH_D = TC // 2
    SUM_D, SUM_P = TOP * CH_D, TOP
    YB = 4
    LD_EX = NE * 2 * 16
    LD_R = 11 * 16

    with ExitStack() as ctx:
        def sb(name, shape, dt=F32, stack=ctx):
            return stack.enter_context(nc.sbuf_tensor(name, shape, dt))

        def sem(name):
            return ctx.enter_context(nc.semaphore(name))

        x_all = sb("x_all", [P, NCH, D])
        idn = sb("idn", [P, P])
        minus_half = sb("minus_half", [P, TC])
        stats = sb("stats", [P, 2, TC, 6])
        moments = sb("moments", [P, 2, TC, 2])
        var_eps = sb("var_eps", [P, 2, TC])
        rstd = sb("rstd", [P, 2, TC])
        xt = sb("xt", [P, S])
        keys_sb = sb("keys_sb", [P, NE])
        rw_sb = sb("rw_sb", [P, NE])
        keys2 = sb("keys2", [P, NE])
        rk = sb("rk", [P, NE])
        lrow = sb("lrow", [P, NE])
        lconst = sb("lconst", [P, NE])
        ones = sb("ones", [P, P])
        eno = sb("eno", [P, NE])
        region_sb = sb("region_sb", [P, NE])
        carry = sb("carry", [P, NE])
        home_sb = sb("home_sb", [P, NCH, TOP])
        pad_sb = sb("pad_sb", [P, BC * (D + 1)])
        blkno_sb = sb("blkno_sb", [1, NTAB])
        upto_sb = sb("upto_sb", [1, NE, NE])
        par_at = sb("par_at", [1, NTAB], I32)
        row_at = sb("row_at", [1, NTAB], I32)
        nblk = sb("nblk", [1, NSEG])
        nblk_i = sb("nblk_i", [1, NE], I32)
        fill = sb("fill", [1, NE], I32)
        ends16 = sb("ends16", [1, NE])
        jump16 = sb("jump16", [1, NE])
        eob = sb("eob", [1, EARLY])
        hops16 = sb("hops16", [1, EARLY])
        lg = sb("lg", [P, TC, NE])
        top = sb("top", [P, TC, 8])
        idx = sb("idx", [P, TC, 8], U32)
        idxf = sb("idxf", [P, TC, TOP])
        diff = sb("diff", [P, TC, TOP])
        ev = sb("ev", [P, TC, TOP])
        esum = sb("esum", [P, TC])
        einv = sb("einv", [P, TC])
        wt = sb("wt", [P, NCH, TOP])
        picked = sb("picked", [P, TC, TOP, NE])
        mask = sb("mask", [P, TC, NE], BF16)
        ones_bf = sb("ones_bf", [P, P], BF16)
        before_bf = sb("before_bf", [P, P], BF16)
        free = sb("free", [P, TC, NE])
        slotf = sb("slotf", [P, TC, TOP])
        slot = sb("slot", [P, TC * TOP], I32)
        copies = sb("copies", [P, TC, 2, D + 1])

        PROBS = 2 * 2 * TC * S
        AHEAD = max(0, NE * EW - H * STRIP - PROBS // 2)
        shared = sb("shared", [P, AHEAD + H * STRIP + PROBS])
        strips = shared[:, AHEAD:AHEAD + H * STRIP].rearrange("p (h m) -> p h m", h=H)
        prob = shared[:, AHEAD + H * STRIP:].rearrange("p (a b c s) -> p a b c s", a=2, b=2, c=TC)
        params = shared[:, 0:NE * EW]

        attn = ctx.enter_context(ExitStack())
        xn = xt[:].rearrange("p (c d) -> p c d", c=TC)
        xnt_hi = sb("xnt_hi", [P, S], F32R, attn)
        xnt_lo = sb("xnt_lo", [P, S], F32R, attn)
        w_hi = [sb(f"w{n}_hi", [P, H * DH], F32R, attn)[:] for n in "kqv"]
        w_lo = [sb(f"w{n}_lo", [P, H * DH], F32R, attn)[:] for n in "kqv"]
        wo_sb = sb("wo_sb", [P, NPR, D], stack=attn)
        rb_sb = sb("rb_sb", [NBUCKET, H], stack=attn)
        q_st = sb("q_st", [P, 2, 2, S], F32R, attn)
        k_st = sb("k_st", [P, 2, 2, S], F32R, attn)
        k_sw = sb("k_sw", [P, 2, 2, S], F32R, attn)
        v_sb = sb("v_sb", [P, 2, TC, VW], stack=attn)
        neg = sb("neg", [P, 2, S], stack=attn)
        nmax = sb("nmax", [P, TILES], stack=attn)
        rsum = sb("rsum", [P, TILES], stack=attn)
        rinv = sb("rinv", [P, TILES], stack=attn)
        probt = sb("probt", [P, 2, TC, S], stack=attn)
        ctxt = sb("ctxt", [P, 2, S], stack=attn)
        stage = [probt[:, 0, 2 * n:2 * n + 2, :].rearrange("p a m -> p (a m)") for n in range(2)] + \
                [probt[:, 1, 0:2, :].rearrange("p a m -> p (a m)")]
        scratch = shared[:, AHEAD + H * STRIP:]
        onehot_sb = scratch[0:NBUCKET, 0:ROLL].rearrange("p (a m) -> p a m", a=2)
        roll_sb = scratch[0:H, ROLL:2 * ROLL].rearrange("p (a m) -> p a m", a=2)
        late = scratch[:, PROBS // 2:]
        before_sb = late[:, 0:P]
        far_sb = late[:, P:P + 2 * H].rearrange("p (a h) -> p a h", a=2)

        roll_dram = nc.dram_tensor("roll_dram", [H, ROLL], F32, kind="Internal").ap()
        xs_dram = nc.dram_tensor("xs_dram", [NE * REGION + BLK, D + 1], F32, kind="Internal").ap()
        y_dram = nc.dram_tensor("y_dram", [TOP * T, D], F32, kind="Internal").ap()
        y_rows = y_dram.rearrange("(n p k c) d -> n p k c d", p=P, k=TOP, c=TC)

        banks = [ctx.enter_context(nc.psum_tensor(f"bank{n}", [P, 512], F32)) for n in range(8)]
        ps_prj, ps_s, ps_t, ps_c, ps_o = banks[0:2], banks[2:4], banks[4:6], banks[6], banks[7]

        ld_x0, ld_x1, ld_x, ld_c, ld_w = sem("ld_x0"), sem("ld_x1"), sem("ld_x"), sem("ld_c"), [sem(f"ld_w{n}") for n in "kqv"]
        ld_wo, roll_st, ld_strip = sem("ld_wo"), sem("roll_st"), [sem(f"ld_strip{g}") for g in range(H // TC)]
        ld_r, one_rdy, bf_rdy = sem("ld_r"), sem("one_rdy"), sem("bf_rdy")
        w_hi_rdy, w_lo_rdy = sem("w_hi_rdy"), sem("w_lo_rdy")
        roll_mm, roll_cp = sem("roll_mm"), sem("roll_cp")
        far_mm, far_cp, far_rdy, far_late = sem("far_mm"), sem("far_cp"), sem("far_rdy"), sem("far_late")
        half_rdy = sem("half_rdy")
        st_rdy, mv_rdy, ve_rdy, rstd_rdy, xn_rdy = (sem(n) for n in ("st_rdy", "mv_rdy", "ve_rdy", "rstd_rdy", "xn_rdy"))
        xt_rdy, xhi_rdy, xlo_rdy = sem("xt_rdy"), sem("xhi_rdy"), sem("xlo_rdy")
        k_rdy, q_rdy, v_rdy = sem("k_rdy"), sem("q_rdy"), sem("v_rdy")
        hi_rdy, lo_rdy, v_cp = sem("hi_rdy"), sem("lo_rdy"), sem("v_cp")
        ksw_rdy = [sem("ksw_rdy0"), sem("ksw_rdy1")]
        s_rdy, neg_rdy, exp_rdy, rinv_rdy, norm_rdy = (sem(n) for n in
                                                       ("s_rdy", "neg_rdy", "exp_rdy", "rinv_rdy", "norm_rdy"))
        t_rdy, pt_act, pt_dve = sem("t_rdy"), sem("pt_act"), sem("pt_dve")
        c_rdy, c_cp, o_rdy, res_rdy = sem("c_rdy"), sem("c_cp"), sem("o_rdy"), sem("res_rdy")
        k2_rdy, kk_rdy, rk_rdy, lc_rdy = sem("k2_rdy"), sem("kk_rdy"), sem("rk_rdy"), sem("lc_rdy")
        st2, mv2, ve2, rstd2, xn2 = (sem(n) for n in ("st2", "mv2", "ve2", "rstd2", "xn2"))
        xt2_rdy, xcp_rdy, l_rdy, lg_rdy, top_rdy, idx_rdy = (sem(n) for n in (
            "xt2_rdy", "xcp_rdy", "l_rdy", "lg_rdy", "top_rdy", "idx_rdy"))
        diff_rdy, idxf_rdy, ev_rdy, es_rdy, ei_rdy, wt_rdy = (sem(n) for n in (
            "diff_rdy", "idxf_rdy", "ev_rdy", "es_rdy", "ei_rdy", "wt_rdy"))
        pick_rdy, mask_rdy, rank_rdy, free_rdy, carry_rdy, sel_rdy, slotf_rdy, slot_rdy = (sem(n) for n in (
            "pick_rdy", "mask_rdy", "rank_rdy", "free_rdy", "carry_rdy", "sel_rdy", "slotf_rdy", "slot_rdy"))
        copy_rdy, sent = sem("copy_rdy"), [sem("sent_even"), sem("sent_odd")]
        ld_ex, tab, at_rdy = sem("ld_ex"), sem("tab"), sem("at_rdy")

        def far_strips(a, first, end):
            return strips[:, first:end, a * (FAR + NEAR):a * (FAR + NEAR) + FAR]

        def far_bias(a, first, end):
            return far_sb[:, a, first:end].unsqueeze(2).broadcast_to([P, end - first, FAR])

        def bank_v(i):
            return ps_prj[(3 * i) % 2]

        def bank_kq(i, n):
            return ps_prj[(3 * i + 1 + n) % 2]

        def pair_piece(i, m):
            return bank_kq(i, m % 2), (k_st, q_st)[m % 2], m // 2

        def next_pair(b, i):
            return (b, i + 1) if i + 1 < NPR else (b + 1, 0)

        def before(b, i, k):
            return (b, i - k) if i >= k else (b - 1, i - k + NPR)

        def run_steps(eng, step, drain):
            for i in range(NPR):
                step(0, i)
            with eng.Fori(1, LAST) as b:
                for i in range(NPR):
                    step(b, i)
            for i in range(NPR):
                step(LAST, i)
            drain()

        def exists(b):
            return not (isinstance(b, int) and b < 0)

        def ends(b):
            return isinstance(b, int) and b == LAST

        def is_last(b, i):
            return ends(b) and i == NPR - 1

        def route_act(act, n, stage_no):
            if stage_no == 0:
                act.wait_ge(xt2_rdy, n + 1)
                act.activation(xt[:], ps_c[:], ACT.Copy).then_inc(xcp_rdy, 1)
            else:
                act.wait_ge(diff_rdy, n + 1)
                act.activation(ev[:], diff[:], ACT.Exp).then_inc(ev_rdy, 1)

        def route_pe(pe, n, stage_no):
            if stage_no == 0:
                pe.wait_ge(xn2, (n + 1) * TC)
                for c in range(TC):
                    mm = pe.transpose(ps_c[:, c * P:(c + 1) * P], copies[:, c, 0, 0:D], idn[:])
                mm.then_inc(xt2_rdy, 1)
            elif stage_no == 1:
                pe.wait_ge(xcp_rdy, n + 1)
                for c in range(TC):
                    mm = pe.matmul(ps_c[:, c * NE:(c + 1) * NE], xt[:, c * P:(c + 1) * P], rk[:], start=True, stop=True)
                mm.then_inc(l_rdy, 1)
            else:
                pe.wait_ge(mask_rdy, n + 1)
                pe.matmul(ps_c[:, 0:TC * NE], before_bf[:], mask[:].rearrange("p c e -> p (c e)"),
                          start=True, stop=False, skip_group_check=True)
                for c in range(TC):
                    mm = pe.matmul(ps_c[:, (c + 1) * NE:(TC + 1) * NE], ones_bf[:],
                                   mask[:, c:c + 1, :].broadcast_to([P, TC - c, NE]),
                                   start=False, stop=True, skip_group_check=True)
                mm.then_inc(rank_rdy, 1)

        SCATTERS = TC * TOP
        SENT = SCATTERS // 2 * 16

        def route_pool(pool, n, stage_no):
            if stage_no == "rstd":
                pool.wait_ge(ve2, n + 1)
                pool.tensor_tensor(rstd[:, 1], var_eps[:, 1], minus_half[:], ALU.pow).then_inc(rstd2, 1)
            elif stage_no == "copy":
                pool.wait_ge(xn2, (n + 1) * TC)
                pool.nop(nofuse=True)
                pool.tensor_copy(copies[:, :, 1, 0:D], copies[:, :, 0, 0:D]).then_inc(copy_rdy, 1)
                pool.tensor_copy(copies[:, :, :, D], home_sb[:, bass.ds(n * TC, TC), 0:2]).then_inc(copy_rdy, 1)
            else:
                k, c = stage_no // TC, stage_no % TC
                if stage_no == 0:
                    pool.wait_ge(copy_rdy, n * 4 + 2)
                    pool.wait_ge(slot_rdy, n + 1)
                    pool.nop(nofuse=True)
                if k >= 2 and c == 0:
                    pool.wait_ge(sent[k % 2], n * SENT + SENT // 2)
                    pool.nop(nofuse=True)
                    pool.tensor_copy(copies[:, :, k % 2, D:D + 1], home_sb[:, bass.ds(n * TC, TC), k:k + 1])\
                        .then_inc(copy_rdy, 1)
                    pool.wait_ge(copy_rdy, n * 4 + k + 1)
                    pool.nop(nofuse=True)
                pool.indirect_dma_start(xs_dram, bass.IndirectOffsetOnAxis(
                    ap=slot[:, c * TOP + k:c * TOP + k + 1], axis=0), copies[:, c, k % 2, :], None).then_inc(sent[k % 2], 16)

        def moments_of(dve, n, q, stage_no, st, mv, ve):
            if stage_no == 0:
                for c in range(TC):
                    dve.bn_stats(stats[:, q, c, :], x_all[:, bass.ds(n * TC + c, 1), :]).then_inc(st, 1)
            elif stage_no == 1:
                dve.wait_ge(st, (n + 1) * TC)
                dve.nop(nofuse=True)
                for c in range(TC):
                    dve.bn_aggr(moments[:, q, c, :], stats[:, q, c, :]).then_inc(mv, 1)
            else:
                dve.wait_ge(mv, (n + 1) * TC)
                dve.tensor_scalar(var_eps[:, q], moments[:, q, :, 1], EPS, None, ALU.add).then_inc(ve, 1)

        def normalise(dve, n, q, to, ready, done):
            dve.wait_ge(ready, n + 1)
            for c in range(TC):
                dve.tensor_scalar(to[:, c, :], x_all[:, bass.ds(n * TC + c, 1), :], moments[:, q, c, 0:1],
                                  rstd[:, q, c:c + 1], ALU.subtract, ALU.mult).then_inc(done, 1)

        def route_dve(dve, n, stage_no):
            if stage_no == 0:
                dve.wait_ge(res_rdy, n + 1)
                dve.nop(nofuse=True)
            if stage_no < 3:
                moments_of(dve, n, 1, stage_no, st2, mv2, ve2)
            elif stage_no == 3:
                normalise(dve, n, 1, copies[:, :, 0, 0:D], rstd2, xn2)
            elif stage_no == 4:
                dve.wait_ge(l_rdy, n + 1)
                dve.tensor_tensor(lg[:], ps_c[:, 0:TC * NE].rearrange("p (c e) -> p c e", e=NE),
                                  lconst[:].unsqueeze(1).broadcast_to([P, TC, NE]), ALU.add).then_inc(lg_rdy, 1)
            elif stage_no == 5:
                dve.wait_ge(lg_rdy, n + 1)
                dve.nop(nofuse=True)
                for c in range(TC):
                    dve.max(top[:, c, :], lg[:, c, :]).then_inc(top_rdy, 1)
            elif stage_no == 6:
                dve.wait_ge(top_rdy, (n + 1) * TC)
                dve.nop(nofuse=True)
                for c in range(TC):
                    dve.max_index(idx[:, c, :], top[:, c, :], lg[:, c, :]).then_inc(idx_rdy, 1)
                dve.tensor_tensor(diff[:], top[:, :, 0:TOP], top[:, :, 0:1].broadcast_to([P, TC, TOP]),
                                  ALU.subtract).then_inc(diff_rdy, 1)
            elif stage_no == 7:
                dve.wait_ge(idx_rdy, (n + 1) * TC)
                dve.tensor_copy(idxf[:], idx[:, :, 0:TOP]).then_inc(idxf_rdy, 1)
            elif stage_no == 8:
                dve.wait_ge(idxf_rdy, n + 1)
                dve.tensor_tensor(picked[:], eno[:].unsqueeze(1).unsqueeze(1).broadcast_to([P, TC, TOP, NE]),
                                  idxf[:].unsqueeze(3).broadcast_to([P, TC, TOP, NE]), ALU.is_equal).then_inc(pick_rdy, 1)
            elif stage_no == 9:
                dve.wait_ge(pick_rdy, n + 1)
                with nc.allow_low_precision(reason="zeros and ones, exact"):
                    dve.tensor_reduce(mask[:], picked[:].rearrange("p c k e -> p c e k"), AX.X, ALU.add).then_inc(mask_rdy, 1)
            elif stage_no == 10:
                dve.wait_ge(ev_rdy, n + 1)
                dve.tensor_reduce(esum[:], ev[:], AX.X, ALU.add).then_inc(es_rdy, 1)
            elif stage_no == 11:
                dve.wait_ge(es_rdy, n + 1)
                dve.reciprocal(einv[:], esum[:]).then_inc(ei_rdy, 1)
            elif stage_no == 12:
                dve.wait_ge(ei_rdy, n + 1)
                dve.tensor_tensor(wt[:, bass.ds(n * TC, TC), :], ev[:], einv[:].unsqueeze(2).broadcast_to([P, TC, TOP]),
                                  ALU.mult).then_inc(wt_rdy, 1)
            elif stage_no == 13:
                dve.wait_ge(rank_rdy, n + 1)
                dve.tensor_tensor(free[:], ps_c[:, 0:TC * NE].rearrange("p (c e) -> p c e", e=NE),
                                  carry[:].unsqueeze(1).broadcast_to([P, TC, NE]), ALU.add).then_inc(free_rdy, 1)
            elif stage_no == 14:
                dve.wait_ge(free_rdy, n + 1)
                dve.tensor_tensor(carry[:], ps_c[:, TC * NE:(TC + 1) * NE], carry[:], ALU.add).then_inc(carry_rdy, 1)
                dve.wait_ge(mask_rdy, n + 1)
                dve.tensor_tensor(picked[:], picked[:], free[:].unsqueeze(2).broadcast_to([P, TC, TOP, NE]),
                                  ALU.mult).then_inc(sel_rdy, 1)
            elif stage_no == 15:
                dve.wait_ge(sel_rdy, n + 1)
                dve.tensor_reduce(slotf[:], picked[:], AX.X, ALU.add).then_inc(slotf_rdy, 1)
            else:
                dve.wait_ge(slotf_rdy, n + 1)
                dve.tensor_copy(slot[:], slotf[:].rearrange("p c k -> p (c k)")).then_inc(slot_rdy, 1)
                dve.wait_ge(carry_rdy, n + 1)

        ROUTE_STAGES = 17
        def early_table(dve, stage_no):
            cum = picked[0:1].rearrange("p c k e -> p (c k e)")[:, 0:NE * NE].rearrange("p (a b) -> p a b", a=NE)
            past = xt[0:1, 0:EARLY * NE].rearrange("p (n e) -> p n e", e=NE)
            if stage_no == 0:
                dve.scalar_tensor_tensor(fill[:], carry[0:1, :], 0.0, region_sb[0:1, :], ALU.add, ALU.subtract)\
                    .then_inc(tab, 1)
                dve.wait_ge(tab, 1)
                dve.tensor_scalar(nblk_i[:], fill[:], BLK.bit_length() - 1, None, ALU.logical_shift_right).then_inc(tab, 1)
                dve.wait_ge(tab, 2)
                dve.tensor_copy(nblk[:, 0:NE], nblk_i[:]).then_inc(tab, 1)
            elif stage_no == 1:
                dve.wait_ge(tab, 3)
                dve.tensor_tensor(cum, upto_sb[:], nblk[:, 0:NE].unsqueeze(1).broadcast_to([1, NE, NE]), ALU.mult)\
                    .then_inc(tab, 1)
                dve.tensor_scalar(jump16[:], nblk[:, 0:NE], float(-BLK), float(REGION), ALU.mult, ALU.add).then_inc(tab, 1)
                dve.wait_ge(tab, 5)
                dve.tensor_reduce(ends16[:], cum, AX.X, ALU.add).then_inc(tab, 1)
            elif stage_no == 2:
                dve.wait_ge(tab, 6)
                dve.tensor_tensor(past, blkno_sb[:, 0:EARLY].unsqueeze(2).broadcast_to([1, EARLY, NE]),
                                  ends16[:].unsqueeze(1).broadcast_to([1, EARLY, NE]), ALU.is_ge).then_inc(tab, 1)
            elif stage_no == 3:
                dve.wait_ge(tab, 7)
                dve.tensor_reduce(eob[:], past, AX.X, ALU.add).then_inc(tab, 1)
            elif stage_no == 4:
                dve.wait_ge(tab, 8)
                dve.tensor_scalar(par_at[:, 0:EARLY], eob[:], float(NE - 1), float(EW), ALU.min, ALU.mult).then_inc(at_rdy, 1)
                dve.tensor_tensor(past, past, jump16[:].unsqueeze(1).broadcast_to([1, EARLY, NE]), ALU.mult).then_inc(tab, 1)
            else:
                dve.wait_ge(tab, 9)
                dve.tensor_reduce(hops16[:], past, AX.X, ALU.add).then_inc(tab, 1)
                dve.wait_ge(tab, 10)
                dve.scalar_tensor_tensor(row_at[:, 0:EARLY], blkno_sb[:, 0:EARLY], float(BLK), hops16[:], ALU.mult, ALU.add)\
                    .then_inc(at_rdy, 1)

        EARLY_TABLE = {(6, 1): 0, (6, 3): 1, (6, 5): 2, (6, 7): 3, (7, 4): 4, (7, 6): 5}
        ROUTE_DVE = {(2, 1): (0,), (2, 5): (1, 2), (3, 0): (3,), (4, 2): (4,), (4, 5): (5,), (5, 0): (6, 7, 8, 9), (5, 1): (10,),
                     (5, 2): (11, 13), (5, 3): (14,), (5, 5): (12, 15), (5, 6): (16,)}
        ROUTE_PE = {(3, 2): 0, (4, 1): 1, (5, 1): 2}
        ROUTE_ACT = {(3, 3): 0, (5, 1): 1}
        ROUTE_POOL = {(2, 3): "rstd", (3, 1): "copy"}
        ROUTE_POOL.update({(5 + (4 + q) // TILES, (4 + q) % TILES): q for q in range(SCATTERS)})

        phase = ctx.enter_context(ExitStack())
        block = phase.enter_context(nc.Block())

        @block.sync
        def _(sp):
            sp.dma_start(rb_sb[:], rel_bias).then_inc(ld_c, 16)
            sp.dma_start(onehot_sb, onehot.rearrange("n (a m) -> n a m", a=2)).then_inc(ld_c, 16)
            sp.dma_start(x_all[:, 0:TC, :], x[0:S].rearrange("(n p) d -> p n d", p=P)).then_inc(ld_x0, 16)
            sp.dma_start(idn[:], ident).then_inc(ld_c, 16)
            for n, w in enumerate((wk, wq, wv)):
                sp.dma_start(stage[n], w).then_inc(ld_w[n], 16)
            sp.wait_ge(roll_cp, 2)
            sp.dma_start(roll_dram.rearrange("h (a m) -> h a m", a=2), roll_sb).then_inc(roll_st, 16)
            sp.wait_ge(roll_st, 16)
            def swap(b, i):
                for hh in range(2):
                    sp.wait_ge(lo_rdy, b * PIECES + 4 * i + 2 * hh + 1)
                    sp.dma_start(k_sw[0:DH, i % 2, hh].bitcast(F32), k_st[DH:P, i % 2, hh].bitcast(F32))\
                        .then_inc(ksw_rdy[hh], 16)
                    sp.dma_start(k_sw[DH:P, i % 2, hh].bitcast(F32), k_st[0:DH, i % 2, hh].bitcast(F32))\
                        .then_inc(ksw_rdy[hh], 16)

            def load_strips(g):
                sp.dma_start(strips[:, g * TC:(g + 1) * TC, FAR:FAR + NEAR],
                             bass.AP(roll_dram.tensor, g * TC * ROLL + FAR, [[1, P], [ROLL, TC], [1, NEAR]]))\
                    .then_inc(ld_strip[g], 16)

            def load_expert(e):
                sp.dma_start(params[:, e * EW:e * EW + B2], experts[e]).then_inc(ld_ex, 16)
                sp.dma_start(params[:, e * EW + B2:(e + 1) * EW], b2[e:e + 1, :].broadcast_to([P, D])).then_inc(ld_ex, 16)

            load_strips(0)
            swap(0, 0)
            sp.dma_start(x_all[:, TC:2 * TC, :], x[S:2 * S].rearrange("(n p) d -> p n d", p=P)).then_inc(ld_x1, 16)
            for to, src in ((keys_sb, keys_t), (rw_sb, rw_t), (lrow, rb.broadcast_to([P, NE])), (eno, expert_no), (before_sb, before_tok),
                            (region_sb, region), (carry, region), (home_sb, home_row.rearrange("p (n k) -> p n k", k=TOP)),
                            (pad_sb, pad), (blkno_sb, block_no),
                            (upto_sb, upto.rearrange("o (a b) -> o a b", a=NSEG)[:, 0:NE, 0:NE])):
                sp.dma_start(to[:], src).then_inc(ld_r, 16)
            swap(0, 1)
            load_strips(1)
            sp.dma_start(wo_sb[:], wo.rearrange("(n p) d -> p n d", p=P)).then_inc(ld_wo, 16)
            for i in range(2, NPR):
                swap(0, i)
                if i <= H // TC - 1:
                    load_strips(i)
                else:
                    for n in range(2 * (i - H // TC) + 2, min(2 * (i - H // TC) + 4, NB)):
                        sp.dma_start(x_all[:, n * TC:(n + 1) * TC, :],
                                     x[n * S:(n + 1) * S].rearrange("(n p) d -> p n d", p=P)).then_inc(ld_x, 16)
            with sp.Fori(1, LAST) as b:
                for i in range(NPR):
                    swap(b, i)
            free_to = [AHEAD + 2 * STRIP * (i + 1) for i in range(NPR)] + [AHEAD + H * STRIP + PROBS // 2]
            e = 0
            for i in range(NPR + 3):
                if i < NPR:
                    swap(LAST, i)
                if i >= 2:
                    if i - 2 < NPR:
                        sp.wait_ge(neg_rdy, LAST * CHUNKS + (i - 1) * TILES)
                    else:
                        sp.wait_ge(t_rdy, LAST * CHUNKS + (NPR - 1) * TILES)
                    while e < NE and (e + 1) * EW <= free_to[i - 2]:
                        load_expert(e)
                        e += 1

        @block.gpsimd
        def _(pool):
            pool.memset(minus_half[:], -0.5).then_inc(half_rdy, 1)
            pool.memset(ones[:], 1.0).then_inc(one_rdy, 1)
            pool.memset(ones_bf[:], 1.0).then_inc(one_rdy, 1)
            pool.wait_ge(half_rdy, 1)

            def rsqrt(n):
                pool.wait_ge(ve_rdy, n + 1)
                pool.tensor_tensor(rstd[:, 0], var_eps[:, 0], minus_half[:], ALU.pow).then_inc(rstd_rdy, 1)

            def step(b, i):
                for n in range(TILES):
                    if n % 2 == 0:
                        pool.wait_ge(rinv_rdy, b * (CHUNKS // 2) + (TILES * i + n) // 2 + 1)
                        pool.nop(nofuse=True)
                    tile = prob[:, i % 2, n // TC, n % TC, :]
                    pool.tensor_scalar(tile, tile, rinv[:, n:n + 1], 1.0, ALU.mult, ALU.mult).then_inc(norm_rdy, 1)
                    if i == 3 and n == 0 and not ends(b):
                        rsqrt(b + 1)
                    if (i, n) in ROUTE_POOL and exists(b - 1):
                        route_pool(pool, b - 1, ROUTE_POOL[i, n])
                if i == NPR - 1 and exists(b - 1):
                    for parity in range(2):
                        pool.wait_ge(sent[parity], b * SENT)
                    pool.nop(nofuse=True)

            rsqrt(0)
            pool.wait_ge(far_cp, 1)
            for a in range(2):
                pool.tensor_copy(far_strips(a, H // 2, H), far_bias(a, H // 2, H)).then_inc(far_late, 1)
            pool.wait_ge(ld_r, LD_R)
            run_steps(pool, step, lambda: None)

        @block.scalar
        def _(act):
            def tokens_hi(n):
                act.wait_ge(xt_rdy, n + 1)
                act.activation(xnt_hi[:], ps_c[:], ACT.Copy).then_inc(xhi_rdy, 1)

            def split_hi(b, i, m):
                src, dst, hh = pair_piece(i, m)
                nb, ni = next_pair(b, i)
                act.wait_ge(q_rdy if m % 2 else k_rdy, nb * NPR + ni + 1)
                act.activation(dst[0:DH, ni % 2, hh, :], src[DH * hh:DH * hh + DH, :], ACT.Copy).then_inc(hi_rdy, 1)

            def values(b, i):
                act.wait_ge(v_rdy, b * NPR + i + 1)
                act.activation(v_sb[:, i // 2 % 2, 2 * (i % 2):2 * (i % 2) + 2, :].rearrange("p c d -> p (c d)"), bank_v(i)[:],
                               ACT.Copy).then_inc(v_cp, 1)

            def exps(b, i, n):
                act.wait_ge(neg_rdy, b * CHUNKS + TILES * i + n + 1)
                act.activation(prob[:, i % 2, n // TC, n % TC, :], neg[:, n % 2, :], ACT.Exp,
                               bias=nmax[:, n:n + 1], scale=-1.0, accum_out=rsum[:, n:n + 1]).then_inc(exp_rdy, 1)

            def weights_t(b, i, hh, j):
                act.wait_ge(t_rdy, b * CHUNKS + TILES * i + TC * hh + j + 1)
                act.activation(probt[:, hh, j, :], ps_t[j % 2][:], ACT.Copy).then_inc(pt_act, 1)

            def context(b, i):
                act.wait_ge(c_rdy, b * NPR + i + 1)
                act.activation(ctxt[:, i % 2, ::-1], ps_c[:], ACT.Copy).then_inc(c_cp, 1)

            HI = {2: 0, 3: 1, 5: 2, 6: 3}
            HI_LATE = {3: 0, 4: 1, 5: 2, 6: 3}

            def step(b, i):
                hi = HI_LATE if i == NPR - 1 else HI
                for n in range(TILES):
                    if n == 0 and exists(before(b, i, 2)[0]):
                        context(*before(b, i, 2))
                    if n == 1 and i == NPR - 1 and not ends(b):
                        tokens_hi(b + 1)
                    if 1 <= n <= TC and exists(before(b, i, 1)[0]):
                        weights_t(*before(b, i, 1), (n - 1) // 2, 2 * ((n - 1) % 2) + 1)
                    if n == 1:
                        values(b, i)
                    if (i, n) in ROUTE_ACT and exists(b - 1):
                        route_act(act, b - 1, ROUTE_ACT[i, n])
                    if n in hi and not is_last(b, i):
                        split_hi(b, i, hi[n])
                    exps(b, i, n)

            def drain():
                context(LAST, NPR - 2)
                for hh in range(2):
                    weights_t(LAST, NPR - 1, hh, 1)
                    weights_t(LAST, NPR - 1, hh, 3)
                context(LAST, NPR - 1)

            def weights_hi(n):
                act.wait_ge(ld_w[n], 16)
                act.activation(w_hi[n], stage[n], ACT.Copy).then_inc(w_hi_rdy, 1)

            weights_hi(0)
            weights_hi(1)
            act.wait_ge(far_mm, 1)
            act.activation(far_sb, ps_t[0][:, 0:2 * H].rearrange("p (a h) -> p a h", a=2), ACT.Copy).then_inc(far_cp, 1)
            tokens_hi(0)
            for a in range(2):
                act.wait_ge(roll_mm, a + 1)
                act.activation(roll_sb[:, a, :], ps_s[a][0:H, :], ACT.Copy).then_inc(roll_cp, 1)
            weights_hi(2)
            act.wait_ge(far_cp, 1)
            act.activation(far_strips(0, 0, H // 2), far_bias(0, 0, H // 2), ACT.Copy).then_inc(far_rdy, 1)
            for m in range(4):
                split_hi(-1, NPR - 1, m)
            run_steps(act, step, drain)

        @block.vector
        def _(dve):
            def tokens_lo(n):
                dve.wait_ge(xhi_rdy, n + 1)
                dve.tensor_tensor(xnt_lo[:], ps_c[:], xnt_hi[:].bitcast(F32), ALU.subtract).then_inc(xlo_rdy, 1)

            def split_lo(b, i, m):
                src, dst, hh = pair_piece(i, m)
                nb, ni = next_pair(b, i)
                dve.wait_ge(hi_rdy, nb * PIECES + 4 * ni + m + 1)
                dve.tensor_tensor(dst[DH:P, ni % 2, hh, :], src[DH * hh:DH * hh + DH, :],
                                  dst[0:DH, ni % 2, hh, :].bitcast(F32), ALU.subtract).then_inc(lo_rdy, 1)

            def scores(b, i, n):
                m = TILES * i + n
                if not (isinstance(b, int) and b * CHUNKS + m < 2):
                    dve.wait_ge(exp_rdy, b * CHUNKS + m - 1)
                dve.wait_ge(s_rdy, b * CHUNKS + m + 1)
                dve.nop(nofuse=True)
                shift = n % TC * P
                if isinstance(b, int) and b == 0 and n == 0:
                    if i % (TC // 2) == 0:
                        dve.wait_ge(ld_strip[2 * i // TC], 16)
                    if i == 1:
                        dve.wait_ge(far_late, 2)
                    dve.nop(nofuse=True)
                dve.tensor_tensor_reduce(neg[:, n % 2, :], ps_s[n % 2][:],
                                         strips[:, 2 * i + n // TC, shift:shift + S],
                                         -1.0, BIG, ALU.add, ALU.min, nmax[:, n:n + 1]).then_inc(neg_rdy, 1)

            def reciprocal(b, i, n):
                dve.wait_ge(exp_rdy, b * CHUNKS + TILES * i + n + 2)
                dve.reciprocal(rinv[:, n:n + 2], rsum[:, n:n + 2]).then_inc(rinv_rdy, 1)

            def weights_t(b, i, hh, j):
                dve.wait_ge(t_rdy, b * CHUNKS + TILES * i + TC * hh + j + 1)
                dve.tensor_copy(probt[:, hh, j, :], ps_t[j % 2][:]).then_inc(pt_dve, 1)

            def residual(b):
                dve.wait_ge(o_rdy, (b + 1) * NPR)
                dve.tensor_tensor(x_all[:, bass.ds(b * TC, TC), :], ps_o[:].rearrange("p (c d) -> p c d", c=TC),
                                  x_all[:, bass.ds(b * TC, TC), :], ALU.add).then_inc(res_rdy, 1)

            LO = {3: (0,), 4: (1,), 6: (2,), 7: (3,)}
            LO_LATE = {4: (0,), 5: (1,), 6: (2,), 7: (3,)}
            NEXT = {(0, 5): 0, (1, 5): 1, (2, 4): 2}

            CONSTANTS = {(0, 7): 0, (2, 3): 1}

            def routing_constants(part):
                if part == 0:
                    dve.wait_ge(ld_r, LD_R)
                    dve.tensor_copy(before_bf[:], before_sb).then_inc(bf_rdy, 1)
                    dve.tensor_tensor(keys2[:], keys_sb[:], keys_sb[:], ALU.mult).then_inc(k2_rdy, 1)
                    dve.scalar_tensor_tensor(rk[:], keys_sb[:], 2.0, rw_sb[:], ALU.mult, ALU.add).then_inc(rk_rdy, 1)
                else:
                    dve.wait_ge(kk_rdy, 1)
                    dve.tensor_tensor(lconst[:], lrow[:], ps_c[:, 0:NE], ALU.subtract).then_inc(lc_rdy, 1)

            def step(b, i):
                lo = LO_LATE if i == NPR - 1 else LO
                for n in range(TILES):
                    scores(b, i, n)
                    if n == 0 and i == 2 and exists(b - 1):
                        residual(b - 1)
                    if n == 0 and exists(before(b, i, 1)[0]):
                        reciprocal(*before(b, i, 1), TILES - 2)
                    if n in (2, 4, 6):
                        reciprocal(b, i, n - 2)
                    if i == NPR - 2 and n == 5 and not ends(b):
                        normalise(dve, b + 1, 0, xn, rstd_rdy, xn_rdy)
                    if i == NPR - 1 and n == 1 and not ends(b):
                        tokens_lo(b + 1)
                    if isinstance(b, int) and b == 0:
                        if (i, n) in CONSTANTS:
                            routing_constants(CONSTANTS[i, n])
                        if (i, n) == (0, 5):
                            dve.wait_ge(ld_x1, 16)
                        if (i, n) == (NPR - 1, 0):
                            dve.wait_ge(ld_x, 16 * (NB - 2))
                    if (i, n) in NEXT and not ends(b):
                        moments_of(dve, b + 1, 0, NEXT[i, n], st_rdy, mv_rdy, ve_rdy)
                    if not is_last(b, i):
                        for m in lo.get(n, ()):
                            split_lo(b, i, m)
                    if exists(b - 1):
                        for stage_no in ROUTE_DVE.get((i, n), ()):
                            route_dve(dve, b - 1, stage_no)
                    if (i, n) in EARLY_TABLE and ends(b):
                        early_table(dve, EARLY_TABLE[i, n])
                    if n < TC and exists(before(b, i, 1)[0]):
                        weights_t(*before(b, i, 1), n // 2, 2 * (n % 2))

            def drain():
                reciprocal(LAST, NPR - 1, TILES - 2)
                for hh in range(2):
                    weights_t(LAST, NPR - 1, hh, 0)
                    weights_t(LAST, NPR - 1, hh, 2)
                residual(LAST)

            dve.wait_ge(ld_x0, 16)
            for stage_no in range(3):
                moments_of(dve, 0, 0, stage_no, st_rdy, mv_rdy, ve_rdy)
            normalise(dve, 0, 0, xn, rstd_rdy, xn_rdy)
            for n in range(3):
                dve.wait_ge(w_hi_rdy, n + 1)
                dve.tensor_tensor(w_lo[n], stage[n], w_hi[n].bitcast(F32), ALU.subtract).then_inc(w_lo_rdy, 1)
                if n == 0:
                    tokens_lo(0)
            dve.wait_ge(far_cp, 1)
            dve.tensor_copy(far_strips(1, 0, H // 2), far_bias(1, 0, H // 2)).then_inc(far_rdy, 1)
            for m in range(4):
                split_lo(-1, NPR - 1, m)
            dve.wait_ge(far_rdy, 2)
            run_steps(dve, step, drain)

        @block.tensor
        def _(pe):
            def tokens_t(n):
                pe.wait_ge(xn_rdy, (n + 1) * TC)
                for c in range(TC):
                    mm = pe.transpose(ps_c[:, c * P:(c + 1) * P], xn[:, c, :], idn[:])
                mm.then_inc(xt_rdy, 1)

            def three(to, a_hi, a_lo, b_hi, b_lo):
                pe.matmul(to, a_lo, b_hi, start=True, stop=False)
                pe.matmul(to, a_hi, b_lo, start=False, stop=False)
                return pe.matmul(to, a_hi, b_hi, start=False, stop=True)

            def project(i, n):
                ni = (i + 1) % NPR
                cols = slice(ni * P, (ni + 1) * P)
                order = slice(None, None, -1 if n else 1)
                three(bank_kq(i, n)[:], w_hi[n][:, cols], w_lo[n][:, cols], xnt_hi[:, order], xnt_lo[:, order])\
                    .then_inc((k_rdy, q_rdy)[n], 1)

            def project_v(i):
                cols = slice(i // 2 * VW, (i // 2 + 1) * VW)
                for a in range(2):
                    c = 2 * (i % 2) + a
                    tok = slice(c * P, (c + 1) * P)
                    mm = three(bank_v(i)[:, a * VW:(a + 1) * VW], xnt_hi[:, tok], xnt_lo[:, tok],
                               w_hi[2][:, cols], w_lo[2][:, cols])
                mm.then_inc(v_rdy, 1)

            def scores(b, i, n):
                m = TILES * i + n
                if not (isinstance(b, int) and b * CHUNKS + m < 2):
                    pe.wait_ge(neg_rdy, b * CHUNKS + m - 1)
                if n % TC == 0:
                    pe.wait_ge(lo_rdy, b * PIECES + 4 * i + 2 * (n // TC) + 2)
                    pe.wait_ge(ksw_rdy[n // TC], b * (32 * NPR) + 32 * (i + 1))
                q = q_st[:, i % 2, n // TC, (n % TC) * P:(n % TC + 1) * P]
                pe.matmul(ps_s[n % 2][:], q, k_st[:, i % 2, n // TC, :], start=True, stop=False)
                pe.matmul(ps_s[n % 2][:], q, k_sw[:, i % 2, n // TC, :], start=False, stop=True).then_inc(s_rdy, 1)

            def weights_t(b, i, hh, j):
                m = TILES * i + TC * hh + j
                if j == 0:
                    pe.wait_ge(norm_rdy, b * CHUNKS + TILES * i + TC * (hh + 1))
                if not (isinstance(b, int) and b * CHUNKS + m < 2):
                    pe.wait_ge(pt_act if j % 2 else pt_dve, b * (CHUNKS // 2) + m // 2)
                for c in range(TC):
                    mm = pe.transpose(ps_t[j % 2][:, c * P:(c + 1) * P], prob[:, i % 2, hh, c, j * P:(j + 1) * P], idn[:])
                mm.then_inc(t_rdy, 1)

            def weigh(b, i, j):
                if j == 0:
                    pe.wait_ge(v_cp, b * NPR + i - i % 2 + 2)
                    if not (isinstance(b, int) and b == 0 and i == 0):
                        pe.wait_ge(c_cp, b * NPR + i)
                pe.wait_ge(pt_act if j % 2 else pt_dve, b * (CHUNKS // 2) + TC * i + 2 + j // 2 + 1)
                for hh in range(2):
                    col = (i % 2) * P + DH * hh
                    mm = pe.matmul(ps_c[DH * hh:DH * hh + DH, :], v_sb[:, i // 2 % 2, j, col:col + DH],
                                   probt[:, hh, j, :], start=(j == 0), stop=(j == TC - 1))
                if j == TC - 1:
                    mm.then_inc(c_rdy, 1)

            def project_out(b, i, c):
                if c == 0:
                    pe.wait_ge(c_cp, b * NPR + i + 1)
                    if i == 0 and exists(b - 1):
                        pe.wait_ge(res_rdy, b)
                mm = pe.matmul(ps_o[:, c * P:(c + 1) * P], ctxt[:, i % 2, c * P:(c + 1) * P], wo_sb[:, i, :],
                               start=(i == 0 and c == 0), stop=(i == NPR - 1), skip_group_check=True)
                if c == TC - 1:
                    mm.then_inc(o_rdy, 1)

            def step(b, i):
                one, two = before(b, i, 1), before(b, i, 2)
                late = i == NPR - 1
                for n in range(TILES):
                    if isinstance(b, int) and b == 0 and (i, n) == (2, 2):
                        pe.wait_ge(one_rdy, 2)
                        pe.wait_ge(k2_rdy, 1)
                        pe.wait_ge(c_cp, 1)
                        pe.matmul(ps_c[:, 0:NE], ones[:], keys2[:], start=True, stop=True).then_inc(kk_rdy, 1)
                    if isinstance(b, int) and b == 0 and (i, n) == (2, TC):
                        pe.wait_ge(ld_wo, 16)
                        pe.wait_ge(rk_rdy, 1)
                        pe.wait_ge(lc_rdy, 1)
                        pe.wait_ge(bf_rdy, 1)
                    if n + 1 < TILES:
                        scores(b, i, n + 1)
                    elif not is_last(b, i):
                        scores(*next_pair(b, i), 0)
                    if n == 0:
                        pe.wait_ge(lo_rdy, b * PIECES + 4 * i + 3)
                        project_v(i)
                    if n == 0 and late and not ends(b):
                        pe.wait_ge(c_cp, b * NPR + i - 1)
                        tokens_t(b + 1)
                    if (i, n) in ROUTE_PE and exists(b - 1):
                        pe.wait_ge(c_cp, b * NPR + i - 1)
                        route_pe(pe, b - 1, ROUTE_PE[i, n])
                    if n == 1 and not late:
                        pe.wait_ge(lo_rdy, b * PIECES + 4 * i + 4)
                        project(i, 0)
                    if n < TC and exists(one[0]):
                        weights_t(*one, n // 2, 2 * (n % 2))
                        weights_t(*one, n // 2, 2 * (n % 2) + 1)
                    if n == 2 and late and not ends(b):
                        pe.wait_ge(lo_rdy, b * PIECES + 4 * i + 4)
                        pe.wait_ge(xlo_rdy, b + 2)
                        project(i, 0)
                    if n == (3 if late else 2) and not is_last(b, i):
                        pe.wait_ge(v_cp, b * NPR + i + 1)
                        project(i, 1)
                    if n == TC and exists(b - 1):
                        if i == 3:
                            pe.wait_ge(xcp_rdy, b)
                        if i == 4:
                            pe.wait_ge(lg_rdy, b)
                        if i == 5:
                            pe.wait_ge(carry_rdy, b)
                    if n >= TC and exists(one[0]):
                        weigh(*one, n - TC)
                    if n >= TC and exists(two[0]):
                        project_out(*two, n - TC)

            def drain():
                for c in range(TC):
                    project_out(LAST, NPR - 2, c)
                for hh in range(2):
                    for j in range(TC):
                        weights_t(LAST, NPR - 1, hh, j)
                for j in range(TC):
                    weigh(LAST, NPR - 1, j)
                for c in range(TC):
                    project_out(LAST, NPR - 1, c)

            pe.wait_ge(ld_c, 48)
            for a in range(2):
                pe.matmul(ps_s[a][0:H, :], rb_sb[:], onehot_sb[:, a, :], start=True, stop=True).then_inc(roll_mm, 1)
            for a, m in ((0, 0), (1, ROLL // 2 - 1)):
                mm = pe.matmul(ps_t[0][:, a * H:(a + 1) * H], onehot_sb[:, a, m:m + 1].broadcast_to([NBUCKET, P]), rb_sb[:],
                               start=True, stop=True)
            mm.then_inc(far_mm, 1)
            tokens_t(0)
            pe.wait_ge(xlo_rdy, 1)
            for n in range(2):
                pe.wait_ge(w_lo_rdy, n + 1)
                project(NPR - 1, n)
            pe.wait_ge(w_lo_rdy, 3)
            pe.wait_ge(roll_cp, 2)
            pe.wait_ge(far_cp, 1)
            scores(0, 0, 0)
            run_steps(pe, step, drain)

        phase.close()
        attn.close()
        pad_at = sb("pad_at", [1, NE], I32)
        upto_all = sb("upto_all", [1, NSEG, NSEG])
        seg_sb = sb("seg_sb", [1, NSEG + 1])
        step_sb = sb("step_sb", [1, NSEG])
        nall = sb("nall", [1, NE])
        cum = sb("cum", [1, NSEG, NSEG])
        ends = sb("ends", [1, NSEG])
        gap = sb("gap", [1, NSEG])
        jump = sb("jump", [1, NSEG])
        past = sb("past", [1, NTAB - EARLY, NSEG])
        steps = sb("steps", [1, NTAB - EARLY, NSEG])
        stepf = sb("stepf", [1, NTAB - EARLY])
        hops = sb("hops", [1, NTAB - EARLY])
        rowf = sb("rowf", [1, NTAB - EARLY])
        warm = sb("warm", [P, TC])
        xb = sb("xb", [P, UN, BC, D + 1])
        yb = sb("yb", [P, UN, BC, D])
        home = sb("home", [P, UN, BC], I32)
        xbt_hi = sb("xbt_hi", [P, 2, BLK], F32R)
        xbt_lo = sb("xbt_lo", [P, 2, BLK], F32R)
        w1_hi = sb("w1_hi", [P, 2, F], F32R)
        w1_lo = sb("w1_lo", [P, 2, F], F32R)
        act_h = sb("act_h", [P, 2, FC, BLK])
        yk = shared[:, 0:YB * TOP * S].rearrange("p (a k c d) -> p a k c d", k=TOP, c=TC, d=D)
        ps_xt, ps_y, ps_h = banks[0], banks[1], (banks[2:4], banks[4:6])

        def hidden_bank(q, f):
            return ps_h[q % 2][f // BCH][:, f % BCH * BLK:(f % BCH + 1) * BLK]

        ld_pad = sem("ld_pad")
        ld_tab, tab2, pad_rdy, pads_sent = (sem(n) for n in ("ld_tab", "tab2", "pad_rdy", "pads_sent"))
        ld_xb = [sem(f"ld_xb{j}") for j in range(UN)]
        xbt_rdy, xbhi_rdy, xblo_rdy, w1hi_rdy, w1lo_rdy = (sem(n) for n in (
            "xbt_rdy", "xbhi_rdy", "xblo_rdy", "w1hi_rdy", "w1lo_rdy"))
        hh_rdy, gelu_rdy = sem("hh_rdy"), sem("gelu_rdy")
        y_mm, home_rdy, yb_rdy = sem("y_mm"), sem("home_rdy"), sem("yb_rdy")
        y_sent = [sem(f"y_sent{j}") for j in range(UN)]
        ld_y = [[sem(f"ld_y{a}_{k}") for k in range(TOP)] for a in range(YB)]
        weighed, sum_d, sum_p = sem("weighed"), sem("sum_d"), sem("sum_p")
        st_out = sem("st_out")

        def starts(m, lag):
            return not isinstance(m, int) or m >= lag

        def run_blocks(eng, step, drain, regs=None, table=None, rest=None):
            def keep():
                for j in range(LAG if regs else 0):
                    eng.reg_mov(regs[j], regs[UN + j])

            def load(it):
                for q in range(0, UN if regs else 0, 4):
                    eng.load(regs[LAG + q:LAG + q + 4], table[0:1, bass.ds(it * UN + q, 4)])

            for it in range(PEEL // UN):
                if it:
                    keep()
                load(it)
                for j in range(UN):
                    step(it * UN + j, j)
            for first, end in ((PEEL // UN, EARLY // UN), (EARLY // UN, REST)):
                if first == EARLY // UN and rest:
                    rest()
                with eng.Fori(first, end) as it:
                    keep()
                    load(it)
                    for j in range(UN):
                        step(it * UN + j, j)
            keep()
            load(REST)
            for j in range(END):
                step(REST * UN + j, j)
            drain()

        TAIL_PE = {1: 0, 2: 1, 4: 2}
        TAIL_ACT = {1: 0, 3: 1}
        TAIL_DVE = {2: (4, 5, 6), 3: (7, 8, 9), 4: (10, 11, 13, 14), 5: (12, 15, 16)}
        TAIL_POOL = {m: (2 * m - 4, 2 * m - 3) for m in range(2, 2 + SCATTERS // 2)}
        TAIL_TABLE = {6 + n: n for n in range(8)}
        PADS = 12

        block = ctx.enter_context(nc.Block())

        @block.sync
        def _(sp):
            def load_table():
                sp.dma_start(xs_dram[NE * REGION:NE * REGION + BLK, :].rearrange("(p c) d -> p (c d)", c=BC), pad_sb[:])\
                    .then_inc(ld_pad, 16)
                for to, src in ((upto_all, upto.rearrange("o (a b) -> o a b", a=NSEG)), (seg_sb, seg_row), (step_sb, par_step)):
                    sp.dma_start(to[:], src).then_inc(ld_tab, 16)

            ends_at = [sp.alloc_register(f"end{e}") for e in range(4)]
            rows = [sp.alloc_register(f"row{j}") for j in range(LAG + UN)]

            def fill_up():
                sp.wait_ge(pad_rdy, 1)
                for e in range(NE):
                    if e % 4 == 0:
                        sp.load(ends_at, pad_at[0:1, e:e + 4])
                    end = sp.snap(ends_at[e % 4], min_val=0, max_val=NE * REGION - BLK)
                    sp.dma_start(xs_dram[bass.ds(end, BLK), :].rearrange("(p c) d -> p (c d)", c=BC), pad_sb[:])\
                        .then_inc(pads_sent, 16)

            def step(m, j):
                if isinstance(m, int) and m == UN:
                    load_table()
                if isinstance(m, int) and m == PADS:
                    fill_up()
                if not isinstance(m, int) or m >= UN:
                    sp.wait_ge(xbt_rdy, m - UN + 1)
                    sp.wait_ge(home_rdy, m - UN + 1)
                row = sp.snap(rows[LAG + j], min_val=0, max_val=NE * REGION)
                sp.dma_start(xb[:, j], xs_dram[bass.ds(row, BLK), :].rearrange("(p c) d -> p c d", c=BC)).then_inc(ld_xb[j], 16)

            def rest():
                sp.wait_ge(at_rdy, 4)
                sp.wait_ge(ld_pad, 16)
                for parity in range(2):
                    sp.wait_ge(sent[parity], NB * SENT)
                sp.wait_ge(pads_sent, NE * 16)

            sp.wait_ge(at_rdy, 2)
            for parity in range(2):
                sp.wait_ge(sent[parity], LAST * SENT)
            run_blocks(sp, step, lambda: None, rows, row_at, rest)
            for j in range(UN):
                sp.wait_ge(y_sent[j], BC * 16 * (REST + (1 if j < END else 0)))

            def fetch(n):
                for k in range(TOP):
                    sp.dma_start(yk[:, n % YB, k], y_rows[n, :, k]).then_inc(ld_y[n % YB][k], 16)

            for n in range(YB):
                fetch(n)
            for n in range(NB):
                sp.wait_ge(sum_d, (n + 1) * SUM_D)
                sp.wait_ge(sum_p, (n + 1) * SUM_P)
                sp.dma_start(out[n * S:(n + 1) * S, :].rearrange("(n p) d -> p n d", p=P),
                             x_all[:, n * TC:(n + 1) * TC, :]).then_inc(st_out, 16)
                if n + YB < NB:
                    fetch(n + YB)
            sp.wait_ge(st_out, 16 * NB)

        @block.gpsimd
        def _(pool):
            route_pool(pool, LAST, "rstd")
            route_pool(pool, LAST, "copy")

            def step(m, j):
                pool.wait_ge(home_rdy, m + 1)
                pool.wait_ge(yb_rdy, m + 1)
                pool.nop(nofuse=True)
                for c in range(BC):
                    pool.indirect_dma_start(y_dram, bass.IndirectOffsetOnAxis(ap=home[:, j, c:c + 1], axis=0), yb[:, j, c, :],
                                            None, bounds_check=TOP * T - 1, oob_is_err=False).then_inc(y_sent[j], 16)
                if isinstance(m, int):
                    for q in TAIL_POOL.get(m, ()):
                        route_pool(pool, LAST, q)

            run_blocks(pool, step, lambda: None)
            for n in range(NB):
                here = x_all[:, n * TC + CH_D:(n + 1) * TC, :]
                for k in range(TOP):
                    pool.wait_ge(weighed, (n * TOP + k + 1) * (TC - CH_D))
                    if k:
                        pool.wait_ge(sum_p, n * SUM_P + k)
                    pool.tensor_tensor(here, here, yk[:, n % YB, k, CH_D:TC, :], ALU.add).then_inc(sum_p, 1)

        @block.scalar
        def _(act):
            act.activation(warm[:], minus_half[:], ACT.Gelu)
            act.wait_ge(at_rdy, 2)
            act.wait_ge(ld_ex, LD_EX)

            at = [act.alloc_register(f"a_at{j}") for j in range(LAG + UN)]

            def turned_hi(m, q):
                act.wait_ge(xbt_rdy, m + 1)
                act.activation(xbt_hi[:, q % 2, :], ps_xt[:, 0:BLK], ACT.Copy).then_inc(xbhi_rdy, 1)

            def weights_hi(m, q):
                w = act.snap(at[LAG + q], min_val=0, max_val=(NE - 1) * EW)
                act.activation(w1_hi[:, q % 2, :], params[:, bass.ds(w, F)], ACT.Copy).then_inc(w1hi_rdy, 1)

            def gelu(m, q):
                w = act.snap(at[LAG + q], min_val=0, max_val=(NE - 1) * EW)
                for f in range(FC):
                    if f % BCH == 0:
                        act.wait_ge(hh_rdy, m * (FC // BCH) + f // BCH + 1)
                    act.activation(act_h[:, q % 2, f, :], hidden_bank(q, f), ACT.Gelu,
                                   bias=params[:, bass.ds(w + (B1 + f), 1)]).then_inc(gelu_rdy, 1)

            def step(m, j):
                turned_hi(m, j)
                weights_hi(m, j)
                if isinstance(m, int) and m in TAIL_ACT:
                    route_act(act, LAST, TAIL_ACT[m])
                if starts(m, 1):
                    gelu(m - 1, j - 1)

            def drain():
                gelu(NBLK - 1, END - 1)

            run_blocks(act, step, drain, at, par_at, lambda: act.wait_ge(at_rdy, 4))
            for n in range(NB):
                for k in range(TOP):
                    act.wait_ge(ld_y[n % YB][k], 16 * (n // YB + 1))
                    for c in range(CH_D, TC):
                        rows = yk[:, n % YB, k, c, :]
                        act.activation(rows, rows, ACT.Copy, scale=wt[:, n * TC + c, k:k + 1]).then_inc(weighed, 1)

        @block.vector
        def _(dve):
            def table(stage_no):
                new = slice(NE, NSEG)
                if stage_no == 0:
                    dve.tensor_copy(pad_at[:], carry[0:1, :]).then_inc(pad_rdy, 1)
                    dve.scalar_tensor_tensor(fill[:], carry[0:1, :], float(BLK - 1), region_sb[0:1, :], ALU.add, ALU.subtract)\
                        .then_inc(tab2, 1)
                    dve.wait_ge(tab2, 1)
                    dve.tensor_scalar(nblk_i[:], fill[:], BLK.bit_length() - 1, None, ALU.logical_shift_right).then_inc(tab2, 1)
                    dve.wait_ge(tab2, 2)
                    dve.tensor_copy(nall[:], nblk_i[:]).then_inc(tab2, 1)
                    dve.wait_ge(tab2, 3)
                    dve.tensor_tensor(nblk[:, new], nall[:], nblk[:, 0:NE], ALU.subtract).then_inc(tab2, 1)
                elif stage_no == 1:
                    dve.wait_ge(ld_tab, 16 * 3)
                    dve.scalar_tensor_tensor(seg_sb[:, new], nblk[:, 0:NE], float(BLK), seg_sb[:, new], ALU.mult, ALU.add)\
                        .then_inc(tab2, 1)
                    dve.wait_ge(tab2, 5)
                    dve.tensor_tensor(gap[:], seg_sb[:, 1:NSEG + 1], seg_sb[:, 0:NSEG], ALU.subtract).then_inc(tab2, 1)
                    dve.wait_ge(tab2, 6)
                    dve.scalar_tensor_tensor(jump[:], nblk[:], float(-BLK), gap[:], ALU.mult, ALU.add).then_inc(tab2, 1)
                    dve.tensor_tensor(cum[:], upto_all[:], nblk[:].unsqueeze(1).broadcast_to([1, NSEG, NSEG]), ALU.mult)\
                        .then_inc(tab2, 1)
                elif stage_no == 2:
                    dve.wait_ge(tab2, 8)
                    dve.tensor_reduce(ends[:], cum[:], AX.X, ALU.add).then_inc(tab2, 1)
                elif stage_no == 3:
                    dve.wait_ge(tab2, 9)
                    dve.tensor_tensor(past[:], blkno_sb[:, EARLY:NTAB].unsqueeze(2).broadcast_to([1, NTAB - EARLY, NSEG]),
                                      ends[:].unsqueeze(1).broadcast_to([1, NTAB - EARLY, NSEG]), ALU.is_ge).then_inc(tab2, 1)
                elif stage_no == 4:
                    dve.wait_ge(tab2, 10)
                    dve.tensor_tensor(steps[:], past[:], step_sb[:].unsqueeze(1).broadcast_to([1, NTAB - EARLY, NSEG]), ALU.mult)\
                        .then_inc(tab2, 1)
                elif stage_no == 5:
                    dve.wait_ge(tab2, 11)
                    dve.tensor_reduce(stepf[:], steps[:], AX.X, ALU.add).then_inc(tab2, 1)
                elif stage_no == 6:
                    dve.tensor_tensor(past[:], past[:], jump[:].unsqueeze(1).broadcast_to([1, NTAB - EARLY, NSEG]), ALU.mult)\
                        .then_inc(tab2, 1)
                    dve.wait_ge(tab2, 12)
                    dve.tensor_copy(par_at[:, EARLY:NTAB], stepf[:]).then_inc(at_rdy, 1)
                else:
                    dve.wait_ge(tab2, 13)
                    dve.tensor_reduce(hops[:], past[:], AX.X, ALU.add).then_inc(tab2, 1)
                    dve.wait_ge(tab2, 14)
                    dve.scalar_tensor_tensor(rowf[:], blkno_sb[:, EARLY:NTAB], float(BLK), hops[:], ALU.mult, ALU.add)\
                        .then_inc(tab2, 1)
                    dve.wait_ge(tab2, 15)
                    dve.tensor_scalar(row_at[:, EARLY:NTAB], rowf[:], float(NE * REGION), None, ALU.min).then_inc(at_rdy, 1)

            for stage_no in range(4):
                route_dve(dve, LAST, stage_no)
            at = [dve.alloc_register(f"v_at{j}") for j in range(LAG + UN)]

            def turned_lo(m, q):
                dve.wait_ge(xbhi_rdy, m + 1)
                dve.tensor_tensor(xbt_lo[:, q % 2, :], ps_xt[:, 0:BLK], xbt_hi[:, q % 2, :].bitcast(F32),
                                  ALU.subtract).then_inc(xblo_rdy, 1)

            def weights_lo(m, q):
                w = dve.snap(at[LAG + q], min_val=0, max_val=(NE - 1) * EW)
                dve.wait_ge(w1hi_rdy, m + 1)
                dve.tensor_tensor(w1_lo[:, q % 2, :], params[:, bass.ds(w, F)], w1_hi[:, q % 2, :].bitcast(F32),
                                  ALU.subtract).then_inc(w1lo_rdy, 1)

            def finish(m, q):
                j = q % UN
                w = dve.snap(at[LAG + q], min_val=0, max_val=(NE - 1) * EW)
                dve.wait_ge(ld_xb[j], 16 * ((m - j) // UN + 1) if isinstance(m, int) else (m - j) * (16 // UN) + 16)
                dve.tensor_copy(home[:, j, :], xb[:, j, :, D]).then_inc(home_rdy, 1)
                dve.wait_ge(y_mm, m + 1)
                dve.tensor_tensor(yb[:, j], ps_y[:, 0:BC * D].rearrange("p (c d) -> p c d", d=D),
                                  params[:, bass.ds(w + B2, D)].unsqueeze(1).broadcast_to([P, BC, D]), ALU.add)\
                    .then_inc(yb_rdy, 1)

            def step(m, j):
                if not isinstance(m, int) or m >= UN:
                    dve.wait_ge(y_sent[j], (m - j) * (BC * 16 // UN))
                turned_lo(m, j)
                weights_lo(m, j)
                if isinstance(m, int):
                    for stage_no in TAIL_DVE.get(m, ()):
                        route_dve(dve, LAST, stage_no)
                    if m in TAIL_TABLE:
                        table(TAIL_TABLE[m])
                if starts(m, LAG):
                    finish(m - LAG, j - LAG)

            def drain():
                finish(NBLK - 2, END - 2)
                finish(NBLK - 1, END - 1)

            dve.wait_ge(at_rdy, 2)
            dve.wait_ge(ld_ex, LD_EX)
            run_blocks(dve, step, drain, at, par_at, lambda: dve.wait_ge(at_rdy, 4))
            for n in range(NB):
                for k in range(TOP):
                    dve.wait_ge(ld_y[n % YB][k], 16 * (n // YB + 1))
                    for c in range(CH_D):
                        if k:
                            dve.wait_ge(sum_d, n * SUM_D + (k - 1) * CH_D + c + 1)
                        here = x_all[:, n * TC + c, :]
                        dve.scalar_tensor_tensor(here, yk[:, n % YB, k, c, :], wt[:, n * TC + c, k:k + 1], here,
                                                 ALU.mult, ALU.add).then_inc(sum_d, 1)

        @block.tensor
        def _(pe):
            pe.wait_ge(ld_ex, LD_EX)
            pe.wait_ge(at_rdy, 2)

            at = [pe.alloc_register(f"p_at{j}") for j in range(LAG + UN)]

            def turn(m, q):
                j = q % UN
                if not isinstance(m, int) or m >= 1:
                    pe.wait_ge(xblo_rdy, m)
                pe.wait_ge(ld_xb[j], 16 * (m // UN + 1) if isinstance(m, int) else (m - j) * (16 // UN) + 16)
                for c in range(BC):
                    mm = pe.transpose(ps_xt[:, c * P:(c + 1) * P], xb[:, j, c, 0:D], idn[:])
                mm.then_inc(xbt_rdy, 1)

            def hidden(m, q):
                if not isinstance(m, int) or m >= 2:
                    pe.wait_ge(gelu_rdy, m * FC - FC)
                pe.wait_ge(xblo_rdy, m + 1)
                pe.wait_ge(w1lo_rdy, m + 1)
                hi, lo = xbt_hi[:, q % 2, :], xbt_lo[:, q % 2, :]
                for f in range(FC):
                    to, units = hidden_bank(q, f), slice(f * P, (f + 1) * P)
                    pe.matmul(to, w1_lo[:, q % 2, units], hi, start=True, stop=False)
                    pe.matmul(to, w1_hi[:, q % 2, units], lo, start=False, stop=False)
                    mm = pe.matmul(to, w1_hi[:, q % 2, units], hi, start=False, stop=True)
                    if f % BCH == BCH - 1:
                        mm.then_inc(hh_rdy, 1)

            def second(m, q):
                w = pe.snap(at[LAG + q], min_val=0, max_val=(NE - 1) * EW)
                if not isinstance(m, int) or m >= 1:
                    pe.wait_ge(yb_rdy, m)
                pe.wait_ge(gelu_rdy, m * FC + FC)
                for c in range(BC):
                    for f in range(FC):
                        mm = pe.matmul(ps_y[:, c * D:(c + 1) * D], act_h[:, q % 2, f, c * P:(c + 1) * P],
                                       params[:, bass.ds(w + (W2 + f * D), D)], start=(f == 0), stop=(f == FC - 1))
                mm.then_inc(y_mm, 1)

            def step(m, j):
                turn(m, j)
                if isinstance(m, int) and m in TAIL_PE:
                    if TAIL_PE[m] == 2:
                        pe.wait_ge(lg_rdy, NB)
                    route_pe(pe, LAST, TAIL_PE[m])
                if starts(m, 1):
                    hidden(m - 1, j - 1)
                if starts(m, LAG):
                    second(m - LAG, j - LAG)

            def drain():
                hidden(NBLK - 1, END - 1)
                second(NBLK - 2, END - 2)
                second(NBLK - 1, END - 1)

            run_blocks(pe, step, drain, at, par_at, lambda: pe.wait_ge(at_rdy, 4))


_INS = ["x", "wq", "wk", "wv", "wo", "rel_bias", "onehot", "ident", "expert_no", "before_tok", "region", "home_row", "pad",
         "block_no", "upto", "seg_row", "par_step", "experts", "b2", "keys_t", "rw_t", "rb"]


def kernel(**inputs):
    import math

    import numpy as np
    import concourse.bacc as bacc
    from concourse.bass_utils import run_bass_kernel_spmd

    a = {k: np.asarray(v) for k, v in inputs.items()}
    hs = a["L0_attn_hidden_states"]
    B, S, D = hs.shape
    NBUCKET, H = a["L0_attn_rel_bias"].shape
    E, F, _ = a["L0_ffn_w1"].shape
    f32 = np.float32

    off = np.arange(-(S - 1), S + 1)
    half = NBUCKET // 2
    exact = half // 2
    dist = np.abs(off)
    far = exact + (np.log(np.maximum(dist, 1).astype(f32) / f32(exact)) / f32(math.log(128 / exact))
                   * f32(half - exact)).astype(np.int32)
    bucket = np.where(off > 0, half, 0) + np.where(dist < exact, dist, np.minimum(far, half - 1))
    onehot = (np.arange(NBUCKET)[:, None] == bucket[None, :]).astype(f32)

    batch, chunk = np.divmod(np.arange(B * S // 128), 4)
    home_row = (((batch[:, None] * 128 + np.arange(128)[:, None, None]) * 4 + np.arange(4)) * 4 + chunk[:, None])
    home_row = home_row.astype(f32).reshape(128, -1)
    pad = np.zeros((128, 2, D + 1), f32)
    pad[:, :, D] = 4 * B * S

    arrays = {
        "x": hs.reshape(B * S, D),
        "wq": a["L0_attn_Wq"], "wk": a["L0_attn_Wk"], "wv": a["L0_attn_Wv"], "wo": a["L0_attn_Wo"],
        "rel_bias": a["L0_attn_rel_bias"], "onehot": onehot, "ident": np.eye(128, dtype=f32),
        "expert_no": np.tile(np.arange(E, dtype=f32), (128, 1)),
        "before_tok": np.triu(np.ones((128, 128), f32), 1), "region": np.tile(np.arange(E, dtype=f32) * (B * S + 256), (128, 1)),
        "home_row": home_row, "pad": pad.reshape(128, -1), "block_no": np.arange(B * S * 4 // 256 + E, dtype=f32)[None],
        "upto": np.tril(np.ones((2 * E, 2 * E), f32)).reshape(1, -1),
        "seg_row": np.append(np.tile(np.arange(E, dtype=f32), 2), f32(E))[None] * (B * S + 256),
        "par_step": np.tile(np.append(np.ones(E - 1, f32), f32(1 - E)), 2)[None] * (F * 2 * D // 128 + F // 128 + D),

        "experts": np.concatenate([a["L0_ffn_w1"].transpose(0, 2, 1),
                                   a["L0_ffn_w2"].reshape(E, D, F // 128, 128).transpose(0, 3, 2, 1).reshape(E, 128, -1),
                                   a["L0_ffn_b1"].reshape(E, F // 128, 128).transpose(0, 2, 1)], axis=2),
        "b2": a["L0_ffn_b2"],
        "keys_t": a["L0_ffn_keys"].T, "rw_t": a["L0_ffn_rw"].T,
        "rb": a["L0_ffn_rb"].reshape(1, E),
    }
    arrays = {k: np.ascontiguousarray(v) for k, v in arrays.items()}
    nc = bacc.Bacc("TRN2", target_bir_lowering=False, num_devices=1)
    args = [nc.dram_tensor(f"in_{k}", arrays[k].shape, mybir.dt.from_np(arrays[k].dtype), kind="ExternalInput").ap()
            for k in _INS]
    res = nc.dram_tensor("out_0", (B * S, D), F32, kind="ExternalOutput").ap()
    layer_kernel(nc, *args, res)
    r = run_bass_kernel_spmd(nc, [{f"in_{k}": v for k, v in arrays.items()}], core_ids=[0])
    return r.results[0]["out_0"].reshape(B, S, D)
```
